# Optimizing a Trainium2 kernel written in Bass

```python
import numpy as np
import jax
import jax.numpy as jnp

def _softmax(x, axis=-1):
    return jax.nn.softmax(x, axis=axis)

def _gelu(x):
    return jax.nn.gelu(x, approximate=True)

def _silu(x):
    return jax.nn.silu(x)

def _sigmoid(x):
    return jax.nn.sigmoid(x)

def _layernorm(x, axis=-1, eps=1e-05):
    m = jnp.mean(x, axis=axis, keepdims=True)
    v = jnp.var(x, axis=axis, keepdims=True)
    return (x - m) / jnp.sqrt(v + eps)

def _scatter_add(tgt, idx, src, axis=0):
    return tgt.at[idx].add(src)

def _segment_sum(src, seg, n):
    return jax.ops.segment_sum(src, seg, n)
kernel_name = 'mk_dlrm_tower_d1_rec_r8_78c79f'

def setup_inputs(seed: int=0):
    np.random.seed(seed)
    _w = jnp.asarray

    def _rec_inputs():
        import jax
        import jax.numpy as jnp
        _tk = jax.random.key(seed)
        dense_ctx = jax.random.normal(jax.random.fold_in(_tk, 190), (2048, 16), jnp.float32)
        ids = jnp.stack([jax.random.randint(jax.random.fold_in(_tk, 200 + f), (2048,), 0, v, jnp.int32) for f, v in enumerate([1250, 1250, 125000, 1250, 1250, 1250, 1000, 12500, 1000, 1000, 1250, 125000, 125000, 12500, 12500, 12500, 12500, 1000, 1000, 1250, 1000, 1250, 1250, 12500, 1000, 12500, 1000, 12500, 1000, 1000, 1000, 1000])], axis=1)
        tbl_0 = 0.05 * jax.random.normal(jax.random.fold_in(_tk, 500 + 0), (1250, 64), jnp.float32)
        tbl_1 = 0.05 * jax.random.normal(jax.random.fold_in(_tk, 500 + 1), (1250, 64), jnp.float32)
        tbl_2 = 0.05 * jax.random.normal(jax.random.fold_in(_tk, 500 + 2), (125000, 64), jnp.float32)
        tbl_3 = 0.05 * jax.random.normal(jax.random.fold_in(_tk, 500 + 3), (1250, 64), jnp.float32)
        tbl_4 = 0.05 * jax.random.normal(jax.random.fold_in(_tk, 500 + 4), (1250, 64), jnp.float32)
        tbl_5 = 0.05 * jax.random.normal(jax.random.fold_in(_tk, 500 + 5), (1250, 64), jnp.float32)
        tbl_6 = 0.05 * jax.random.normal(jax.random.fold_in(_tk, 500 + 6), (1000, 64), jnp.float32)
        tbl_7 = 0.05 * jax.random.normal(jax.random.fold_in(_tk, 500 + 7), (12500, 64), jnp.float32)
        tbl_8 = 0.05 * jax.random.normal(jax.random.fold_in(_tk, 500 + 8), (1000, 64), jnp.float32)
        tbl_9 = 0.05 * jax.random.normal(jax.random.fold_in(_tk, 500 + 9), (1000, 64), jnp.float32)
        tbl_10 = 0.05 * jax.random.normal(jax.random.fold_in(_tk, 500 + 10), (1250, 64), jnp.float32)
        tbl_11 = 0.05 * jax.random.normal(jax.random.fold_in(_tk, 500 + 11), (125000, 64), jnp.float32)
        tbl_12 = 0.05 * jax.random.normal(jax.random.fold_in(_tk, 500 + 12), (125000, 64), jnp.float32)
        tbl_13 = 0.05 * jax.random.normal(jax.random.fold_in(_tk, 500 + 13), (12500, 64), jnp.float32)
        tbl_14 = 0.05 * jax.random.normal(jax.random.fold_in(_tk, 500 + 14), (12500, 64), jnp.float32)
        tbl_15 = 0.05 * jax.random.normal(jax.random.fold_in(_tk, 500 + 15), (12500, 64), jnp.float32)
        tbl_16 = 0.05 * jax.random.normal(jax.random.fold_in(_tk, 500 + 16), (12500, 64), jnp.float32)
        tbl_17 = 0.05 * jax.random.normal(jax.random.fold_in(_tk, 500 + 17), (1000, 64), jnp.float32)
        tbl_18 = 0.05 * jax.random.normal(jax.random.fold_in(_tk, 500 + 18), (1000, 64), jnp.float32)
        tbl_19 = 0.05 * jax.random.normal(jax.random.fold_in(_tk, 500 + 19), (1250, 64), jnp.float32)
        tbl_20 = 0.05 * jax.random.normal(jax.random.fold_in(_tk, 500 + 20), (1000, 64), jnp.float32)
        tbl_21 = 0.05 * jax.random.normal(jax.random.fold_in(_tk, 500 + 21), (1250, 64), jnp.float32)
        tbl_22 = 0.05 * jax.random.normal(jax.random.fold_in(_tk, 500 + 22), (1250, 64), jnp.float32)
        tbl_23 = 0.05 * jax.random.normal(jax.random.fold_in(_tk, 500 + 23), (12500, 64), jnp.float32)
        tbl_24 = 0.05 * jax.random.normal(jax.random.fold_in(_tk, 500 + 24), (1000, 64), jnp.float32)
        tbl_25 = 0.05 * jax.random.normal(jax.random.fold_in(_tk, 500 + 25), (12500, 64), jnp.float32)
        tbl_26 = 0.05 * jax.random.normal(jax.random.fold_in(_tk, 500 + 26), (1000, 64), jnp.float32)
        tbl_27 = 0.05 * jax.random.normal(jax.random.fold_in(_tk, 500 + 27), (12500, 64), jnp.float32)
        tbl_28 = 0.05 * jax.random.normal(jax.random.fold_in(_tk, 500 + 28), (1000, 64), jnp.float32)
        tbl_29 = 0.05 * jax.random.normal(jax.random.fold_in(_tk, 500 + 29), (1000, 64), jnp.float32)
        tbl_30 = 0.05 * jax.random.normal(jax.random.fold_in(_tk, 500 + 30), (1000, 64), jnp.float32)
        tbl_31 = 0.05 * jax.random.normal(jax.random.fold_in(_tk, 500 + 31), (1000, 64), jnp.float32)
        _rk = jax.random.fold_in(_tk, 7)
        W_top1 = 0.0441942 * jax.random.normal(jax.random.fold_in(_tk, 801), (512, 512), jnp.float32)
        W_top2 = 0.0441942 * jax.random.normal(jax.random.fold_in(_tk, 802), (512, 256), jnp.float32)
        W_top3 = 0.0625 * jax.random.normal(jax.random.fold_in(_tk, 803), (256, 1), jnp.float32)
        b_top1 = jnp.zeros((512,), jnp.float32)
        b_top2 = jnp.zeros((256,), jnp.float32)
        return (dense_ctx, ids, tbl_0, tbl_1, tbl_2, tbl_3, tbl_4, tbl_5, tbl_6, tbl_7, tbl_8, tbl_9, tbl_10, tbl_11, tbl_12, tbl_13, tbl_14, tbl_15, tbl_16, tbl_17, tbl_18, tbl_19, tbl_20, tbl_21, tbl_22, tbl_23, tbl_24, tbl_25, tbl_26, tbl_27, tbl_28, tbl_29, tbl_30, tbl_31, W_top1, b_top1, W_top2, b_top2, W_top3)
    dense_ctx, ids, tbl_0, tbl_1, tbl_2, tbl_3, tbl_4, tbl_5, tbl_6, tbl_7, tbl_8, tbl_9, tbl_10, tbl_11, tbl_12, tbl_13, tbl_14, tbl_15, tbl_16, tbl_17, tbl_18, tbl_19, tbl_20, tbl_21, tbl_22, tbl_23, tbl_24, tbl_25, tbl_26, tbl_27, tbl_28, tbl_29, tbl_30, tbl_31, W_top1, b_top1, W_top2, b_top2, W_top3 = _rec_inputs()

    def _L0_rec_setup():
        import jax, jax.numpy as jnp
        import numpy as np
        NUM_FIELDS = 32
        BATCH = 2048
        EMBED_DIM = 64
        _pairs = np.array([(i, j) for i in range(NUM_FIELDS - 1) for j in range(i + 1, NUM_FIELDS)], dtype=np.int32)
        ROW = jnp.asarray(_pairs[:, 0])
        COL = jnp.asarray(_pairs[:, 1])
        key = jax.random.key(seed)
        x = jax.random.normal(key, (BATCH, NUM_FIELDS, EMBED_DIM), dtype=jnp.float32)
        return {'x': x}
    _L0_rec_all = _L0_rec_setup()
    _L0_rec_in = {k: v for k, v in _L0_rec_all.items() if k in ()}
    del _L0_rec_all
    return {'dense_ctx': dense_ctx, 'ids': ids, 'tbl_0': tbl_0, 'tbl_1': tbl_1, 'tbl_2': tbl_2, 'tbl_3': tbl_3, 'tbl_4': tbl_4, 'tbl_5': tbl_5, 'tbl_6': tbl_6, 'tbl_7': tbl_7, 'tbl_8': tbl_8, 'tbl_9': tbl_9, 'tbl_10': tbl_10, 'tbl_11': tbl_11, 'tbl_12': tbl_12, 'tbl_13': tbl_13, 'tbl_14': tbl_14, 'tbl_15': tbl_15, 'tbl_16': tbl_16, 'tbl_17': tbl_17, 'tbl_18': tbl_18, 'tbl_19': tbl_19, 'tbl_20': tbl_20, 'tbl_21': tbl_21, 'tbl_22': tbl_22, 'tbl_23': tbl_23, 'tbl_24': tbl_24, 'tbl_25': tbl_25, 'tbl_26': tbl_26, 'tbl_27': tbl_27, 'tbl_28': tbl_28, 'tbl_29': tbl_29, 'tbl_30': tbl_30, 'tbl_31': tbl_31, 'W_top1': W_top1, 'b_top1': b_top1, 'W_top2': W_top2, 'b_top2': b_top2, 'W_top3': W_top3}

def reference(dense_ctx, ids, tbl_0, tbl_1, tbl_2, tbl_3, tbl_4, tbl_5, tbl_6, tbl_7, tbl_8, tbl_9, tbl_10, tbl_11, tbl_12, tbl_13, tbl_14, tbl_15, tbl_16, tbl_17, tbl_18, tbl_19, tbl_20, tbl_21, tbl_22, tbl_23, tbl_24, tbl_25, tbl_26, tbl_27, tbl_28, tbl_29, tbl_30, tbl_31, W_top1, b_top1, W_top2, b_top2, W_top3):
    import jax
    import jax.numpy as jnp

    def _L0_rec_ref(x):
        import jax, jax.numpy as jnp
        import numpy as np
        NUM_FIELDS = 32
        BATCH = 2048
        EMBED_DIM = 64
        _pairs = np.array([(i, j) for i in range(NUM_FIELDS - 1) for j in range(i + 1, NUM_FIELDS)], dtype=np.int32)
        ROW = jnp.asarray(_pairs[:, 0])
        COL = jnp.asarray(_pairs[:, 1])
        s = jnp.sum(x, axis=-1)
        return s[:, ROW] * s[:, COL]
    e = jnp.stack([tbl_0[ids[:, 0]], tbl_1[ids[:, 1]], tbl_2[ids[:, 2]], tbl_3[ids[:, 3]], tbl_4[ids[:, 4]], tbl_5[ids[:, 5]], tbl_6[ids[:, 6]], tbl_7[ids[:, 7]], tbl_8[ids[:, 8]], tbl_9[ids[:, 9]], tbl_10[ids[:, 10]], tbl_11[ids[:, 11]], tbl_12[ids[:, 12]], tbl_13[ids[:, 13]], tbl_14[ids[:, 14]], tbl_15[ids[:, 15]], tbl_16[ids[:, 16]], tbl_17[ids[:, 17]], tbl_18[ids[:, 18]], tbl_19[ids[:, 19]], tbl_20[ids[:, 20]], tbl_21[ids[:, 21]], tbl_22[ids[:, 22]], tbl_23[ids[:, 23]], tbl_24[ids[:, 24]], tbl_25[ids[:, 25]], tbl_26[ids[:, 26]], tbl_27[ids[:, 27]], tbl_28[ids[:, 28]], tbl_29[ids[:, 29]], tbl_30[ids[:, 30]], tbl_31[ids[:, 31]]], axis=1)
    z = _L0_rec_ref(e)
    z = z.reshape(z.shape[0], -1)
    h = jnp.concatenate([z, dense_ctx], axis=1)
    h = jnp.maximum(h @ W_top1 + b_top1, 0.0)
    h = jnp.maximum(h @ W_top2 + b_top2, 0.0)
    y = h @ W_top3
    return y

_drawn_inputs = setup_inputs


def setup_inputs(seed=0):
    import zlib

    import numpy as np

    out = dict(_drawn_inputs(seed))
    spreads = {'b_top1': (0.0, 0.1), 'b_top2': (0.0, 0.1)}
    factors = {}
    for name, (base, spread) in spreads.items():
        noise = np.random.default_rng([zlib.crc32(name.encode()), seed]).standard_normal(out[name].shape)
        drawn = base * np.exp(spread * noise) if base else spread * noise
        out[name] = jnp.asarray(drawn.astype(out[name].dtype))
    for name, factor in factors.items():
        out[name] = (out[name] * factor).astype(out[name].dtype)
    return out
```

```python
from contextlib import ExitStack

import numpy as np

import concourse.bass as bass
from concourse import mybir

F32 = mybir.dt.float32
BF16 = mybir.dt.bfloat16
I32 = mybir.dt.int32
U32 = mybir.dt.uint32
ALU = mybir.AluOpType
ACT = mybir.ActivationFunctionType
AX = mybir.AxisListType

P = 128
BATCH = 2048
D = 64
TILES = BATCH // P
GROUPS = 4
GT = TILES // GROUPS
GB = GT * P

ROWS = [1250, 1250, 125000, 1250, 1250, 1250, 1000, 12500, 1000, 1000, 1250, 125000, 125000, 12500, 12500,
        12500, 12500, 1000, 1000, 1250, 1000, 1250, 1250, 12500, 1000, 12500, 1000, 12500, 1000, 1000, 1000, 1000]
FIELDS = len(ROWS)

NMID = 4
SMALL = sorted((f for f in range(FIELDS) if ROWS[f] < 2000), key=lambda f: -ROWS[f])
MIDDLE = [f for f in range(FIELDS) if 2000 <= ROWS[f] < 20000]
LARGE = [f for f in range(FIELDS) if ROWS[f] >= 20000]
GATHERED = MIDDLE[NMID:] + LARGE
ORDER = SMALL + MIDDLE[:NMID] + GATHERED
NSMALL = len(SMALL)
NSTREAM = NSMALL + NMID
NGATHER = len(GATHERED)

HALF = P // 2
QA, QB = 20, 16
PACKS_A = -(-sum(ROWS[f] > HALF * QB for f in SMALL) // 2)
PACKS_B = -(-(NSMALL - 2 * PACKS_A) // 2)
PACKS = PACKS_A + PACKS_B
NA, NB = 2 * PACKS_A, NSMALL - 2 * PACKS_A
SROWS = PACKS_A * QA + PACKS_B * QB
CA_COLS = NA * QA
SCOLS = CA_COLS + NB * QB
SCOLS_PAD = 2 * SROWS
CHUNKS = 4
CROWS = SROWS // CHUNKS
QM = -(-12500 // P)
SLOT = QM * D
assert SROWS == 2 * QM and SROWS % CHUNKS == 0 and QA * HALF >= 1250 and QB * HALF >= 1000

Q = [QA] * NA + [QB] * NB + [QM] * NMID
FROWS = 3 * NSTREAM + 2
FPAD = 96
ONE = 3 * NSTREAM
assert FROWS <= FPAD

DENSE = 16
H1, H2 = 512, 256
K1 = FIELDS * (FIELDS - 1) // 2 + DENSE
EARLY = K1 // 2
KE = EARLY // P
MT1, MT2 = H1 // P, H2 // P
EARLY_J = next(j for j in range(FIELDS) if DENSE + (j + 1) * j // 2 >= EARLY)
assert EARLY_J == NSMALL + 1 and K1 == 512
MAGIC = 1.5 * 2.0 ** 23


def pair_col(j):
    return DENSE + j * (j - 1) // 2


def pack_span(k):
    if k < PACKS_A:
        return 2 * QA * k, 2 * QA * (k + 1)
    a = CA_COLS + 2 * QB * (k - PACKS_A)
    return a, min(a + 2 * QB, SCOLS)


def hot_items():
    items = [("small", 0), ("small", 1), ("small", 2), ("small", 3)]
    return items + [("mid", k) for k in range(NMID)]


def hot_after(item):
    n = 0
    for it in hot_items():
        n += (PACKS + GT) if it[0] == "small" else 2 * GROUPS
        if it == item:
            return n


def l1_done(u):
    return MT1 * (u + 1) if u < GROUPS else MT1 * GROUPS + (MT1 + MT2) * (u - GROUPS) + MT1


def dlrm_tower(nc, dense, ids, qconst, hotc, maskc, small, mids, big, w1, b1, w2, b2, w3, out):
    ctx = ExitStack()
    with ctx:
        def sb(name, shape, dt):
            return ctx.enter_context(nc.sbuf_tensor(name, shape, dt))

        def ps(name, shape, dt=F32):
            return ctx.enter_context(nc.psum_tensor(name, shape, dt))

        def sem(name):
            return ctx.enter_context(nc.semaphore(name))

        tables = sb("tables", [P, 4 * SLOT], F32)
        small_sb = tables[:, 2 * SLOT:4 * SLOT]
        slot_of = [0, 1, 2, 3, 2]

        def slot(k):
            s = slot_of[k]
            return tables[:, s * SLOT:(s + 1) * SLOT]

        h1part = tables[:, 0:MT1 * BATCH].rearrange("p (m b) -> p m b", m=MT1)
        h1T = tables[:, MT1 * BATCH:MT1 * BATCH + 2 * MT1 * GB].rearrange("p (u m b) -> p u m b", u=2, m=MT1)
        n_id = TILES * NSTREAM

        def tmp(i):
            return tables[:, i * n_id:(i + 1) * n_id].rearrange("p (t f) -> p t f", t=TILES)

        ids_sb = sb("ids_sb", [P, TILES, FIELDS], I32)
        q_sb = sb("q_sb", [P, 2, NSTREAM], F32)
        n_ft = TILES * FPAD // 2
        featA, featB = (tables[:, SLOT + i * n_ft:SLOT + (i + 1) * n_ft].bitcast(BF16).rearrange(
            "p (t f) -> p t f", t=TILES) for i in (0, 1))
        featAT = sb("featAT", [FPAD, BATCH], BF16)
        featBT = sb("featBT", [FPAD, BATCH], BF16)
        hotc_sb = sb("hotc_sb", [FROWS, (PACKS + NMID) * P], BF16)
        maskc_sb = sb("maskc_sb", [FROWS, SCOLS + NMID * QM], BF16)
        ident = sb("ident", [P, P], F32)
        identb = sb("identb", [P, P], BF16)
        sums = sb("sums", [P, SROWS], F32)
        rest = sb("rest", [P, SROWS], F32)
        parts = sb("parts", [P, 3, SCOLS_PAD], BF16)
        msums = sb("msums", [P, QM], F32)
        mrest = sb("mrest", [P, QM], F32)
        mparts = sb("mparts", [P, 2, 3, QM], BF16)
        hot_bytes = 2 * PACKS * GB * 2
        area = sb("area", [P, hot_bytes // 4], F32)
        hots = area[:, :].bitcast(BF16).rearrange("p (u k b) -> p u k b", u=2, k=PACKS)
        zE = area[:, 0:TILES * EARLY].rearrange("p (t k) -> p t k", t=TILES)
        zL = area[:, TILES * EARLY:TILES * EARLY + GT * EARLY].rearrange("p (t k) -> p t k", t=GT)
        hotm = sb("hotm", [P, 2, BATCH], BF16)
        masks = sb("masks", [P, 2, GT, SCOLS], BF16)
        maskm = sb("maskm", [P, 2, TILES, QM], BF16)
        prod = sb("prod", [P, GT, SCOLS], F32)
        prodm = sb("prodm", [P, GT, QM], F32)
        rows = sb("rows", [P, 2, GT * NGATHER, D], F32)
        s = sb("s", [P, TILES, FIELDS], F32)
        dense_sb = sb("dense_sb", [P, TILES, DENSE], F32)
        zT = sb("zT", [P, 2, KE, GB], F32)
        h2T = tables[:, 2 * SLOT:2 * SLOT + MT2 * GB].rearrange("p (m b) -> p m b", m=MT2)
        w1_sb = sb("w1_sb", [P, K1 // P, H1], F32)
        w2_sb = sb("w2_sb", [P, H1 // P, H2], F32)
        w3_sb = sb("w3_sb", [P, H2 // P], F32)
        b1_sb = sb("b1_sb", [P, MT1], F32)
        b2_sb = sb("b2_sb", [P, MT2], F32)
        y_sb = sb("y_sb", [P, TILES], F32)

        psD = ps("psD", [P, 2, 512])
        psL = ps("psL", [P, 2, 512])
        psZ = ps("psZ", [P, 2, 512])
        psH = ps("psH", [P, 2, 512])
        psY = psL[:, 0, 0:TILES]

        d_ids = sem("d_ids")
        d_q = sem("d_q")
        d_const = sem("d_const")
        d_dense = sem("d_dense")
        d_small = [sem(f"d_small{c}") for c in range(CHUNKS)]
        d_mid = [sem(f"d_mid{k}") for k in range(NMID)]
        d_w1 = sem("d_w1")
        d_w2 = sem("d_w2")
        d_vec = sem("d_vec")
        d_rows = [sem(f"d_rows{g}") for g in range(GROUPS)]
        d_out = sem("d_out")
        ident_zero = sem("ident_zero")
        ident_ready = sem("ident_ready")
        chain = sem("chain")
        feat_ready = sem("feat_ready")
        featT_done = sem("featT_done")
        featT_copied = sem("featT_copied")
        dist_done = sem("dist_done")
        hot_done = sem("hot_done")
        small_summed = sem("small_summed")
        mid_summed = sem("mid_summed")
        parts_ready = sem("parts_ready")
        picked = sem("picked")
        taken = sem("taken")
        rows_summed = sem("rows_summed")
        zE_ready = sem("zE_ready")
        zL_ready = sem("zL_ready")
        zT_done = sem("zT_done")
        zT_copied = sem("zT_copied")
        h_done = sem("h_done")
        part_copied = sem("part_copied")
        h1_added = sem("h1_added")
        h1_ready = sem("h1_ready")
        h2_ready = sem("h2_ready")
        y_done = sem("y_done")
        y_copied = sem("y_copied")

        block = ctx.enter_context(nc.Block())

        @block.sync
        def _(sp):
            sp.dma_start(ids_sb[:, :, :], ids).then_inc(d_ids, 16)
            sp.dma_start(q_sb[:, :, :], qconst).then_inc(d_q, 16)
            sp.dma_start(hotc_sb[:, :], hotc).then_inc(d_const, 16)
            sp.dma_start(maskc_sb[:, :], maskc).then_inc(d_const, 16)
            n = CROWS * D
            for c in range(CHUNKS):
                sp.dma_start(small_sb[:, c * n:(c + 1) * n], small[:, c * n:(c + 1) * n]).then_inc(d_small[c], 16)
            for k in range(NMID):
                if k == 0:
                    sp.wait_ge(feat_ready, 2)
                if k == 1:
                    sp.wait_ge(featT_done, 4)
                if k == 2:
                    sp.wait_ge(small_summed, CHUNKS)
                if k == 4:
                    sp.wait_ge(mid_summed, 3)
                sp.dma_start(slot(k), mids[k]).then_inc(d_mid[k], 16)
                if k == 0:
                    sp.dma_start(dense_sb[:, :, :], dense).then_inc(d_dense, 16)
                    sp.dma_start(w1_sb[:, :, :], w1).then_inc(d_w1, 16)
                    sp.dma_start(b1_sb[:, :], b1).then_inc(d_vec, 16)
                    sp.dma_start(b2_sb[:, :], b2).then_inc(d_vec, 16)
                    sp.dma_start(w3_sb[:, :], w3).then_inc(d_vec, 16)
                if k == 2:
                    sp.dma_start(w2_sb[:, :, :], w2).then_inc(d_w2, 16)
            sp.wait_ge(y_copied, 1)
            sp.dma_start(out, y_sb[:, :]).then_inc(d_out, 16)
            sp.wait_ge(d_out, 16)

        @block.gpsimd
        def _(pool):
            pool.memset(ident[:, :], 0.0).then_inc(ident_zero, 1)
            pool.memset(identb[:, :], 0.0).then_inc(ident_zero, 1)
            pool.wait_ge(ident_zero, 2)
            for m in (ident, identb):
                pool.affine_select(out=m[:, :], in_=m[:, :], compare_op=ALU.not_equal, fill=1.0, base=0,
                                   pattern=[[-1, P]], channel_multiplier=1).then_inc(ident_ready, 1)
            pool.wait_ge(d_ids, 16)
            for g in range(GROUPS):
                if g >= 2:
                    pool.wait_ge(rows_summed, g - 1)
                for t in range(GT):
                    for f in range(NGATHER):
                        col = NSTREAM + f
                        pool.indirect_dma_start(
                            out=rows[:, g % 2, t * NGATHER + f, :], out_offset=None, in_=big[f],
                            in_offset=bass.IndirectOffsetOnAxis(
                                ap=ids_sb[:, g * GT + t, col:col + 1].bitcast(U32), axis=0),
                        ).then_inc(d_rows[g], 16)

        @block.scalar
        def _(act):
            for n, (ft, h) in enumerate(((featAT, 0), (featAT, 1), (featBT, 0), (featBT, 1))):
                act.wait_ge(featT_done, n + 1)
                act.activation(ft[:, h * 1024:(h + 1) * 1024], psZ[0:FPAD, n % 2, :].bitcast(BF16),
                               ACT.Copy).then_inc(featT_copied, 1)

            n = 0

            def indicator(dst, cols, rearr=None):
                nonlocal n
                act.wait_ge(dist_done, n + 1)
                src = psD[:, n % 2, 0:cols]
                if rearr:
                    src = src.rearrange("p (t q) -> p t q", t=rearr)
                act.activation(dst, src, ACT.Relu, bias=1.0, scale=-1.0).then_inc(hot_done, 1)
                n += 1

            def small_hots(g):
                if g >= 2:
                    act.wait_ge(picked, GT * (g - 1))
                for k in range(PACKS):
                    indicator(hots[:, g % 2, k, :], GB)
                if g >= 2:
                    act.wait_ge(taken, GT * (g - 1))
                for t in range(GT):
                    indicator(masks[:, g % 2, t, :], SCOLS)

            def mid_hots(k):
                if k >= 2:
                    act.wait_ge(taken, TILES + GROUPS * (k - 1))
                for g in range(GROUPS):
                    indicator(hotm[:, k % 2, g * GB:(g + 1) * GB], GB)
                for g in range(GROUPS):
                    indicator(maskm[:, k % 2, g * GT:(g + 1) * GT, :], GT * QM, GT)

            def copy_zT(u):
                if u >= 2:
                    act.wait_ge(h_done, l1_done(u - 2))
                for c in range(KE):
                    act.wait_ge(zT_done, u * KE + c + 1)
                    act.activation(zT[:, u % 2, c, :], psZ[:, (u * KE + c) % 2, :],
                                   ACT.Copy).then_inc(zT_copied, 1)

            def early_part(u):
                copy_zT(u)
                for m in range(MT1):
                    act.wait_ge(h_done, MT1 * u + m + 1)
                    act.activation(h1part[:, m, u * GB:(u + 1) * GB], psH[:, (MT1 * u + m) % 2, :], ACT.Identity,
                                   bias=b1_sb[:, m:m + 1]).then_inc(part_copied, 1)

            for g in range(GROUPS):
                small_hots(g)
            mid_hots(0)
            mid_hots(1)
            act.wait_ge(d_vec, 48)
            act.wait_ge(mid_summed, 2)
            mid_hots(2)
            early_part(0)
            early_part(1)
            for k in range(3, NMID):
                mid_hots(k)
            early_part(2)
            early_part(3)
            for g in range(GROUPS):
                copy_zT(GROUPS + g)
                for m in range(MT1):
                    act.wait_ge(h1_added, MT1 * g + m + 1)
                    act.activation(h1T[:, g % 2, m, :], h1T[:, g % 2, m, :], ACT.Relu).then_inc(h1_ready, 1)
                if g >= 1:
                    act.wait_ge(y_done, g)
                for m in range(MT2):
                    n_h = l1_done(GROUPS + g) + m
                    act.wait_ge(h_done, n_h + 1)
                    act.activation(h2T[:, m, :], psH[:, n_h % 2, :], ACT.Relu,
                                   bias=b2_sb[:, m:m + 1]).then_inc(h2_ready, 1)
            act.wait_ge(y_done, GROUPS)
            act.activation(y_sb[:, :], psY, ACT.Copy).then_inc(y_copied, 1)

        @block.vector
        def _(dve):
            v = nc.vector
            done = [0]

            def link(ins):
                done[0] += 1
                ins.then_inc(chain, 1)
                dve.wait_ge(chain, done[0])

            link(v.memset(parts[:, :, :], 0.0))
            for ft in (featA, featB):
                link(v.memset(ft[:, :, ONE:FPAD], 0.0))
                link(v.memset(ft[:, :, ONE:ONE + 2], 1.0))
            dve.wait_ge(d_ids, 16)
            dve.wait_ge(d_q, 16)
            idf, hi, lo, a, b = (tmp(i) for i in range(5))
            q_b = q_sb[:, 0, :].unsqueeze(1).to_broadcast([P, TILES, NSTREAM])
            rq_b = q_sb[:, 1, :].unsqueeze(1).to_broadcast([P, TILES, NSTREAM])
            link(v.tensor_copy(idf, ids_sb[:, :, 0:NSTREAM]))
            link(v.scalar_tensor_tensor(out=a, in0=idf, scalar=0.5, in1=rq_b, op0=ALU.add, op1=ALU.mult))
            link(v.tensor_scalar(b, a, -0.5, MAGIC, ALU.add, ALU.add))
            link(v.tensor_scalar_add(hi, b, -MAGIC))
            link(v.tensor_tensor(a, hi, q_b, ALU.mult))
            link(v.tensor_tensor(lo, idf, a, ALU.subtract))
            for n, (x, ft) in enumerate(((hi, featA), (lo, featB))):
                v.tensor_copy(ft[:, :, 0:NSTREAM], x)
                link(v.tensor_tensor(a, x, x, ALU.mult))
                link(v.tensor_copy(ft[:, :, NSTREAM:2 * NSTREAM], a))
                v.tensor_tensor(ft[:, :, 2 * NSTREAM:3 * NSTREAM], a, ft[:, :, NSTREAM:2 * NSTREAM],
                                ALU.subtract).then_inc(feat_ready, 1)
                dve.wait_ge(feat_ready, n + 1)

            for c in range(CHUNKS):
                dve.wait_ge(d_small[c], 16)
                n = CROWS * D
                v.reduce_sum(sums[:, c * CROWS:(c + 1) * CROWS],
                             small_sb[:, c * n:(c + 1) * n].rearrange("p (r d) -> p r d", d=D),
                             axis=AX.X).then_inc(small_summed, 1)
            dve.wait_ge(small_summed, CHUNKS)

            def halves(i, half):
                pp = slice(half * HALF, (half + 1) * HALF)
                na = 2 * QA * PACKS_A
                return (parts[pp, i, 0:na].rearrange("p (k h q) -> p k h q", h=2, q=QA)[:, :, half, :],
                        parts[pp, i, na:SCOLS_PAD].rearrange("p (k h q) -> p k h q", h=2, q=QB)[:, :, half, :])

            def small_rows(x, half):
                pp = slice(half * HALF, (half + 1) * HALF)
                na = QA * PACKS_A
                return (x[pp, 0:na].rearrange("p (k q) -> p k q", q=QA),
                        x[pp, na:SROWS].rearrange("p (k q) -> p k q", q=QB))

            def small_step(op):
                for half in (0, 1):
                    for ab in (0, 1):
                        op(half, ab)

            def sub_step(i, src, dst_of):
                last = None
                for half in (0, 1):
                    for ab in (0, 1):
                        last = v.tensor_tensor(dst_of(half)[ab], small_rows(src, half)[ab], halves(i, half)[ab],
                                               ALU.subtract)
                return last

            def cast_step(i, src):
                last = None
                for half in (0, 1):
                    for ab in (0, 1):
                        last = v.tensor_copy(halves(i, half)[ab], small_rows(src, half)[ab])
                return last

            link(cast_step(0, sums))
            link(sub_step(0, sums, lambda half: small_rows(rest, half)))
            link(cast_step(1, rest))
            sub_step(1, rest, lambda half: halves(2, half)).then_inc(parts_ready, 1)

            for g in range(GROUPS):
                dve.wait_ge(hot_done, hot_after(("small", g)))
                for t in range(GT):
                    n = g * GT + t
                    dve.wait_ge(picked, n + 1)
                    v.tensor_tensor(prod[:, t, :], psL[:, n % 2, 0:SCOLS], masks[:, g % 2, t, :],
                                    ALU.mult).then_inc(taken, 1)
                dve.wait_ge(taken, (g + 1) * GT)
                tt = slice(g * GT, (g + 1) * GT)
                v.reduce_sum(s[:, tt, 0:NA], prod[:, :, 0:CA_COLS].rearrange("p t (f q) -> p t f q", q=QA),
                             axis=AX.X)
                link(v.reduce_sum(s[:, tt, NA:NSMALL],
                                  prod[:, :, CA_COLS:SCOLS].rearrange("p t (f q) -> p t f q", q=QB), axis=AX.X))

            def mid_sums(k):
                dve.wait_ge(d_mid[k], 16)
                v.reduce_sum(msums[:, :], slot(k).rearrange("p (r d) -> p r d", d=D),
                             axis=AX.X).then_inc(mid_summed, 1)
                dve.wait_ge(mid_summed, k + 1)
                if k >= 2:
                    dve.wait_ge(picked, TILES + GROUPS * (k - 1))
                link(v.tensor_copy(mparts[:, k % 2, 0, :], msums[:, :]))
                link(v.tensor_tensor(mrest[:, :], msums[:, :], mparts[:, k % 2, 0, :], ALU.subtract))
                link(v.tensor_copy(mparts[:, k % 2, 1, :], mrest[:, :]))
                v.tensor_tensor(mparts[:, k % 2, 2, :], mrest[:, :], mparts[:, k % 2, 1, :],
                                ALU.subtract).then_inc(parts_ready, 1)

            def mid_take(k):
                dve.wait_ge(hot_done, hot_after(("mid", k)))
                for g in range(GROUPS):
                    n = TILES + GROUPS * k + g
                    dve.wait_ge(picked, n + 1)
                    tt = slice(g * GT, (g + 1) * GT)
                    v.tensor_tensor(prodm[:, :, :], psL[:, n % 2, 0:GT * QM].rearrange("p (t q) -> p t q", t=GT),
                                    maskm[:, k % 2, tt, :], ALU.mult).then_inc(taken, 1)
                    dve.wait_ge(taken, n + 1)
                    link(v.reduce_sum(s[:, tt, NSMALL + k:NSMALL + k + 1], prodm[:, :, :], axis=AX.X))

            def rows_sum(g):
                dve.wait_ge(d_rows[g], 16 * GT * NGATHER)
                v.reduce_sum(s[:, g * GT:(g + 1) * GT, NSTREAM:FIELDS],
                             rows[:, g % 2, :, :].rearrange("p (t f) d -> p t f d", t=GT),
                             axis=AX.X).then_inc(rows_summed, 1)
                dve.wait_ge(rows_summed, g + 1)

            def early_z():
                dve.wait_ge(d_dense, 16)
                v.tensor_copy(zE[:, :, 0:DENSE], dense_sb[:, :, :])
                for j in range(1, EARLY_J + 1):
                    n_i = min(j, EARLY - pair_col(j))
                    last = v.tensor_tensor(zE[:, :, pair_col(j):pair_col(j) + n_i], s[:, :, 0:n_i],
                                           s[:, :, j:j + 1].to_broadcast([P, TILES, n_i]), ALU.mult)
                last.then_inc(zE_ready, 1)

            def late_z(g):
                if g >= 1:
                    dve.wait_ge(zT_done, KE * (GROUPS + g))
                tt = slice(g * GT, (g + 1) * GT)
                for j in range(EARLY_J, FIELDS):
                    i0 = max(0, EARLY - pair_col(j))
                    c = pair_col(j) + i0 - EARLY
                    last = v.tensor_tensor(zL[:, :, c:c + j - i0], s[:, tt, i0:j],
                                           s[:, tt, j:j + 1].to_broadcast([P, GT, j - i0]), ALU.mult)
                last.then_inc(zL_ready, 1)

            mid_sums(0)
            mid_take(0)
            mid_sums(1)
            mid_take(1)
            rows_sum(0)
            early_z()
            for k in range(2, NMID):
                mid_sums(k)
                mid_take(k)
            rows_sum(1)
            for g in range(GROUPS):
                if g >= 2:
                    rows_sum(g)
                late_z(g)
                if g >= 2:
                    dve.wait_ge(h_done, l1_done(GROUPS + g - 2) + MT2)
                for m in range(MT1):
                    n = l1_done(GROUPS + g) - MT1 + m
                    dve.wait_ge(h_done, n + 1)
                    if g == 0 and m == 0:
                        dve.wait_ge(part_copied, MT1 * GROUPS)
                    v.tensor_tensor(h1T[:, g % 2, m, :], psH[:, n % 2, :], h1part[:, m, g * GB:(g + 1) * GB],
                                    ALU.add).then_inc(h1_added, 1)

        @block.tensor
        def _(pe):
            t_ = nc.tensor
            pe.wait_ge(ident_ready, 2)
            for n, ft in enumerate((featA, featA, featB, featB)):
                pe.wait_ge(feat_ready, n // 2 + 1)
                if n >= 2:
                    pe.wait_ge(featT_copied, n - 1)
                o = psZ[0:FPAD, n % 2, :].bitcast(BF16)
                for i in range(8):
                    last = t_.transpose(o[:, i * P:(i + 1) * P], ft[:, (n % 2) * 8 + i, :], identb[:, :])
                last.then_inc(featT_done, 1)
            pe.wait_ge(d_const, 32)
            pe.wait_ge(featT_copied, 4)

            nd = 0

            def dist_bank():
                nonlocal nd
                if nd >= 2:
                    pe.wait_ge(hot_done, nd - 1)
                nd += 1
                return psD[:, (nd - 1) % 2, :]

            def small_dists(g):
                for k in range(PACKS):
                    o = dist_bank()
                    t_.matmul(o, hotc_sb[:, k * P:(k + 1) * P], featAT[0:FROWS, g * GB:(g + 1) * GB],
                              start=True, stop=True).then_inc(dist_done, 1)
                for t in range(GT):
                    o = dist_bank()
                    c = (g * GT + t) * P
                    t_.matmul(o[:, 0:SCOLS], featBT[0:FROWS, c:c + P], maskc_sb[:, 0:SCOLS],
                              start=True, stop=True).then_inc(dist_done, 1)

            def mid_dists(k):
                for g in range(GROUPS):
                    o = dist_bank()
                    t_.matmul(o, hotc_sb[:, (PACKS + k) * P:(PACKS + k + 1) * P],
                              featAT[0:FROWS, g * GB:(g + 1) * GB], start=True, stop=True).then_inc(dist_done, 1)
                for g in range(GROUPS):
                    o = dist_bank()
                    for t in range(GT):
                        c = (g * GT + t) * P
                        last = t_.matmul(o[:, t * QM:(t + 1) * QM], featBT[0:FROWS, c:c + P],
                                         maskc_sb[:, SCOLS + k * QM:SCOLS + (k + 1) * QM], start=True, stop=True)
                    last.then_inc(dist_done, 1)

            def small_pick(g):
                pe.wait_ge(hot_done, hot_after(("small", g)) - GT)
                pe.wait_ge(parts_ready, 1)
                for t in range(GT):
                    n = g * GT + t
                    if n >= 2:
                        pe.wait_ge(taken, n - 1)
                    for k in range(PACKS):
                        c0, c1 = pack_span(k)
                        for i in range(3):
                            last = t_.matmul(psL[:, n % 2, c0:c1], hots[:, g % 2, k, t * P:(t + 1) * P],
                                             parts[:, i, c0:c1], start=(i == 0), stop=(i == 2))
                    last.then_inc(picked, 1)

            def mid_pick(k):
                pe.wait_ge(hot_done, hot_after(("mid", k)) - GROUPS)
                pe.wait_ge(parts_ready, k + 2)
                for g in range(GROUPS):
                    n = TILES + GROUPS * k + g
                    pe.wait_ge(taken, n - 1)
                    for t in range(GT):
                        c = (g * GT + t) * P
                        for i in range(3):
                            last = t_.matmul(psL[:, n % 2, t * QM:(t + 1) * QM], hotm[:, k % 2, c:c + P],
                                             mparts[:, k % 2, i, :], start=(i == 0), stop=(i == 2))
                    last.then_inc(picked, 1)

            def transposes(u, z):
                for c in range(KE):
                    n = u * KE + c
                    if n >= 2:
                        pe.wait_ge(zT_copied, n - 1)
                    for t in range(GT):
                        last = t_.transpose(psZ[:, n % 2, t * P:(t + 1) * P], z[:, t, c * P:(c + 1) * P],
                                            ident[:, :])
                    last.then_inc(zT_done, 1)

            def h_bank_free(n):
                if n < 2:
                    return
                r = n - 2
                if r < MT1 * GROUPS:
                    pe.wait_ge(part_copied, r + 1)
                    return
                g, i = divmod(r - MT1 * GROUPS, MT1 + MT2)
                if i < MT1:
                    pe.wait_ge(h1_added, g * MT1 + i + 1)
                else:
                    pe.wait_ge(h2_ready, g * MT2 + i - MT1 + 1)

            def layer1(u, k0):
                for m in range(MT1):
                    n = l1_done(u) - MT1 + m
                    h_bank_free(n)
                    for c in range(KE):
                        pe.wait_ge(zT_copied, u * KE + c + 1)
                        last = t_.matmul(psH[:, n % 2, :], w1_sb[:, k0 + c, m * P:(m + 1) * P], zT[:, u % 2, c, :],
                                         start=(c == 0), stop=(c == KE - 1))
                    last.then_inc(h_done, 1)

            def early(g):
                transposes(g, zE[:, g * GT:(g + 1) * GT, :])
                layer1(g, 0)

            small_dists(0)
            small_dists(1)
            small_pick(0)
            small_dists(2)
            small_pick(1)
            small_dists(3)
            small_pick(2)
            mid_dists(0)
            small_pick(3)
            mid_dists(1)
            mid_pick(0)
            mid_pick(1)
            mid_dists(2)
            pe.wait_ge(zE_ready, 1)
            pe.wait_ge(d_w1, 16)
            early(0)
            early(1)
            for k in range(3, NMID):
                mid_pick(k - 1)
                mid_dists(k)
            early(2)
            early(3)
            mid_pick(NMID - 1)
            pe.wait_ge(d_w2, 16)
            for g in range(GROUPS):
                pe.wait_ge(zL_ready, g + 1)
                transposes(GROUPS + g, zL)
                layer1(GROUPS + g, KE)
                for m in range(MT2):
                    n = l1_done(GROUPS + g) + m
                    h_bank_free(n)
                    for c in range(MT1):
                        pe.wait_ge(h1_ready, MT1 * g + c + 1)
                        last = t_.matmul(psH[:, n % 2, :], w2_sb[:, c, m * P:(m + 1) * P], h1T[:, g % 2, c, :],
                                         start=(c == 0), stop=(c == MT1 - 1))
                    last.then_inc(h_done, 1)
                pe.wait_ge(h2_ready, MT2 * (g + 1))
                if g == 0:
                    pe.wait_ge(taken, TILES + GROUPS * NMID)
                for t in range(GT):
                    for c in range(MT2):
                        last = t_.matmul(psY[:, g * GT + t:g * GT + t + 1], h2T[:, c, t * P:(t + 1) * P],
                                         w3_sb[:, c:c + 1], start=(c == 0), stop=(c == MT2 - 1))
                last.then_inc(y_done, 1)


def lookup_constants(bf16):
    q = np.array(Q, np.float32)
    qconst = np.ascontiguousarray(np.broadcast_to(np.stack([q, 1.0 / q])[None], (P, 2, NSTREAM)), np.float32)

    def columns(field_of, k_of):
        n = len(k_of)
        c = np.zeros((FROWS, n), np.float32)
        for col in range(n):
            f, k = field_of[col], k_of[col]
            if f is None:
                c[ONE, col] = 4.0
                continue
            c[f, col] = -2.0 * k
            c[NSTREAM + f, col] = 1.0
            c[2 * NSTREAM + f, col] = 1.0
            high = float(np.float32(k * k).astype(bf16))
            c[ONE, col] = high
            c[ONE + 1, col] = k * k - high
        return c.astype(bf16)

    f_hot, k_hot = [], []
    for pack in range(PACKS):
        for half in (0, 1):
            f = 2 * pack + half
            f_hot += [f if f < NSMALL else None] * HALF
            k_hot += list(range(HALF))
    for m in range(NMID):
        f_hot += [NSMALL + m] * P
        k_hot += list(range(P))
    f_mask = [f for f in range(NSTREAM) for _ in range(Q[f])]
    k_mask = [k for f in range(NSTREAM) for k in range(Q[f])]
    return qconst, columns(f_hot, k_hot), columns(f_mask, k_mask)


def kernel(**inputs):
    import ml_dtypes
    import concourse.bacc as _bacc
    from concourse import mybir as _mybir
    from concourse.bass_utils import run_bass_kernel_spmd as _run

    def arr(name):
        return np.asarray(inputs[name])

    def padded(f, parts, q):
        t = arr(f"tbl_{f}")
        full = np.zeros((parts * q, D), t.dtype)
        full[:t.shape[0]] = t
        return full.reshape(parts, q * D)

    qconst, hotc, maskc = lookup_constants(ml_dtypes.bfloat16)
    small = []
    for pack in range(PACKS):
        q = QA if pack < PACKS_A else QB
        pair = [padded(SMALL[f], HALF, q) if f < NSMALL else np.zeros((HALF, q * D), np.float32)
                for f in (2 * pack, 2 * pack + 1)]
        small.append(np.concatenate(pair))
    first = [i * (2 * FIELDS - 1 - i) // 2 for i in range(FIELDS)]
    n_pairs = K1 - DENSE
    rows = list(range(n_pairs, K1))
    for j in range(1, FIELDS):
        for i in range(j):
            a, b = sorted((ORDER[i], ORDER[j]))
            rows.append(first[a] + b - a - 1)
    arrays = {
        "dense": arr("dense_ctx").reshape(P, TILES, DENSE),
        "ids": arr("ids")[:, ORDER].reshape(P, TILES, FIELDS),
        "qconst": qconst, "hotc": hotc, "maskc": maskc,
        "small": np.concatenate(small, axis=1),
    }
    for k in range(NMID):
        arrays[f"mid{k}"] = padded(MIDDLE[k], P, QM)
    for n, f in enumerate(GATHERED):
        arrays[f"big{n}"] = arr(f"tbl_{f}")
    arrays["w1"] = arr("W_top1")[rows].reshape(K1 // P, P, H1).transpose(1, 0, 2)
    arrays["b1"] = arr("b_top1").reshape(MT1, P).T
    arrays["w2"] = arr("W_top2").reshape(MT1, P, H2).transpose(1, 0, 2)
    arrays["b2"] = arr("b_top2").reshape(MT2, P).T
    arrays["w3"] = arr("W_top3").reshape(MT2, P).T
    arrays = {k: np.ascontiguousarray(a) for k, a in arrays.items()}

    nc = _bacc.Bacc("TRN2", target_bir_lowering=False, num_devices=1)
    ap = {k: nc.dram_tensor(f"in_{k}", a.shape, _mybir.dt.from_np(a.dtype), kind="ExternalInput").ap()
          for k, a in arrays.items()}
    out = nc.dram_tensor("out_y", (P, TILES), _mybir.dt.float32, kind="ExternalOutput").ap()
    dlrm_tower(nc, ap["dense"], ap["ids"], ap["qconst"], ap["hotc"], ap["maskc"], ap["small"],
               [ap[f"mid{k}"] for k in range(NMID)], [ap[f"big{n}"] for n in range(NGATHER)],
               ap["w1"], ap["b1"], ap["w2"], ap["b2"], ap["w3"], out)
    r = _run(nc, [{f"in_{k}": a for k, a in arrays.items()}], core_ids=[0])
    return np.asarray(r.results[0]["out_y"]).reshape(BATCH, 1)
```

```python
from contextlib import ExitStack

import numpy as np

import concourse.bass as bass
from concourse import mybir

F32 = mybir.dt.float32
BF16 = mybir.dt.bfloat16
I32 = mybir.dt.int32
U32 = mybir.dt.uint32
ALU = mybir.AluOpType
ACT = mybir.ActivationFunctionType
AX = mybir.AxisListType

P = 128
BATCH = 2048
D = 64
TILES = BATCH // P
GROUPS = 4
GT = TILES // GROUPS
GB = GT * P

ROWS = [1250, 1250, 125000, 1250, 1250, 1250, 1000, 12500, 1000, 1000, 1250, 125000, 125000, 12500, 12500,
        12500, 12500, 1000, 1000, 1250, 1000, 1250, 1250, 12500, 1000, 12500, 1000, 12500, 1000, 1000, 1000, 1000]
FIELDS = len(ROWS)

NMID = 3
SMALL = sorted((f for f in range(FIELDS) if ROWS[f] < 2000), key=lambda f: -ROWS[f])
MIDDLE = [f for f in range(FIELDS) if 2000 <= ROWS[f] < 20000]
LARGE = [f for f in range(FIELDS) if ROWS[f] >= 20000]
GATHERED = LARGE + MIDDLE[NMID:]
NSMALL = len(SMALL)
NSTREAM = NSMALL + NMID
NFIRST = 2
NLAST = len(GATHERED) - NFIRST
ORDER = SMALL + GATHERED[:NFIRST] + MIDDLE[:NMID] + GATHERED[NFIRST:]
MID0 = NSMALL + NFIRST
LAST0 = MID0 + NMID

HALF = P // 2
QA, QB = 20, 16
PACKS_A = -(-sum(ROWS[f] > HALF * QB for f in SMALL) // 2)
PACKS_B = -(-(NSMALL - 2 * PACKS_A) // 2)
PACKS = PACKS_A + PACKS_B
NA, NB = 2 * PACKS_A, NSMALL - 2 * PACKS_A
SROWS = PACKS_A * QA + PACKS_B * QB
CA_COLS = NA * QA
SCOLS = CA_COLS + NB * QB
SCOLS_PAD = 2 * SROWS
CHUNKS = 4
CROWS = SROWS // CHUNKS
QM = -(-12500 // P)
SLOT = QM * D
assert SROWS == 2 * QM and SROWS % CHUNKS == 0 and QA * HALF >= 1250 and QB * HALF >= 1000

Q = [QA] * NA + [QB] * NB + [QM] * NMID
FROWS = 3 * NSTREAM + 2
FPAD = 96
ONE = 3 * NSTREAM
assert FROWS <= FPAD

FEAT_BATCHES = [(0, GT), (GT, TILES - GT)]
FEAT_BANKS = [(0, 0, GT), (1, 0, GT), (0, GT, 6), (0, GT + 6, 6), (1, GT, 6), (1, GT + 6, 6)]
FEAT_NEEDS = [1, 2, 3, 3, 4, 4]

DENSE = 16
H1, H2 = 512, 256
K1 = FIELDS * (FIELDS - 1) // 2 + DENSE
EARLY = K1 // 2
KE = EARLY // P
MT1, MT2 = H1 // P, H2 // P
EARLY_J = next(j for j in range(FIELDS) if DENSE + (j + 1) * j // 2 >= EARLY)
assert EARLY_J == NSMALL + 1 and K1 == 512
MAGIC = 1.5 * 2.0 ** 23


def pair_col(j):
    return DENSE + j * (j - 1) // 2


def pack_span(k):
    if k < PACKS_A:
        return 2 * QA * k, 2 * QA * (k + 1)
    a = CA_COLS + 2 * QB * (k - PACKS_A)
    return a, min(a + 2 * QB, SCOLS)


HOT_ORDER = [("small", 0), ("small", 1), ("mid", 0), ("small", 2), ("small", 3), ("mid", 1)]
HOT_ORDER += [("mid", k) for k in range(2, NMID)]
PICK_ORDER = [("small", g) for g in range(GROUPS)] + [("mid", k) for k in range(NMID)]


def hot_before(item):
    return sum((PACKS + GT) if kind == "small" else 2 * GROUPS for kind, _ in HOT_ORDER[:HOT_ORDER.index(item)])


def hot_after(item):
    return hot_before(item) + ((PACKS + GT) if item[0] == "small" else 2 * GROUPS)


def picks_after(item):
    return GROUPS * (PICK_ORDER.index(item) + 1)


def l1_done(u):
    return MT1 * (u + 1) if u < GROUPS else MT1 * GROUPS + (MT1 + MT2) * (u - GROUPS) + MT1


def dlrm_tower(nc, dense, ids, qconst, hotc, maskc, small, mids, big, w1, b1, w2, b2, w3, out):
    ctx = ExitStack()
    with ctx:
        def sb(name, shape, dt):
            return ctx.enter_context(nc.sbuf_tensor(name, shape, dt))

        def ps(name, shape, dt=F32):
            return ctx.enter_context(nc.psum_tensor(name, shape, dt))

        def sem(name):
            return ctx.enter_context(nc.semaphore(name))

        slots = sb("slots", [P, 2, SLOT], F32)
        lot = sb("lot", [P, 2 * SLOT], F32)
        small_sb = lot[:, :].rearrange("p (r d) -> p r d", d=D)
        h1part = lot[:, 0:MT1 * BATCH].rearrange("p (m b) -> p m b", m=MT1)
        h1T = lot[:, MT1 * BATCH:MT1 * BATCH + 2 * MT1 * GB].rearrange("p (u m b) -> p u m b", u=2, m=MT1)
        n_ft = TILES * FPAD // 2
        featA, featB = (slots[:, 1, i * n_ft:(i + 1) * n_ft].bitcast(BF16).rearrange(
            "p (t f) -> p t f", t=TILES) for i in (0, 1))
        n_id = TILES * NSTREAM
        tmp = [slots[:, 0, i * n_id:(i + 1) * n_id].rearrange("p (t f) -> p t f", t=TILES) for i in range(3)]
        h2T = slots[:, 1, 0:MT2 * GB].rearrange("p (m b) -> p m b", m=MT2)
        zL = slots[:, 1, MT2 * GB:MT2 * GB + GT * EARLY].rearrange("p (t k) -> p t k", t=GT)

        ids_sb = sb("ids_sb", [P, TILES, FIELDS], I32)
        q_sb = sb("q_sb", [P, 2, NSTREAM], F32)
        featAT = sb("featAT", [FPAD, BATCH], BF16)
        featBT = sb("featBT", [FPAD, BATCH], BF16)
        hotc_sb = sb("hotc_sb", [FROWS, (PACKS + NMID) * P], BF16)
        maskc_sb = sb("maskc_sb", [FROWS, SCOLS + NMID * QM], BF16)
        ident = sb("ident", [P, P], F32)
        identb = sb("identb", [P, P], BF16)
        sums = sb("sums", [P, SROWS], F32)
        rest = sb("rest", [P, SROWS], F32)
        parts = sb("parts", [P, 3, SCOLS_PAD], BF16)
        msums = sb("msums", [P, QM], F32)
        mparts = sb("mparts", [P, 2, 3, QM], BF16)
        n_hot = PACKS * GB // 2
        area = sb("area", [P, 2 * n_hot], F32)
        hots = [(area, area, lot, lot)[g][:, g % 2 * n_hot:(g % 2 + 1) * n_hot].bitcast(BF16).rearrange(
            "p (k b) -> p k b", k=PACKS) for g in range(GROUPS)]
        zE = area[:, 0:TILES * EARLY].rearrange("p (t k) -> p t k", t=TILES)
        n_row = GT * NLAST * D
        rows_even = sb("rows_even", [P, GT * NLAST, D], F32)
        rows_odd = area[:, TILES * EARLY:TILES * EARLY + n_row].rearrange("p (r d) -> p r d", d=D)
        rows = [rows_even, rows_odd]
        rows_first = sb("rows_first", [P, TILES * NFIRST, D], F32)
        hotm = sb("hotm", [P, 2, BATCH], BF16)
        masks = sb("masks", [P, 2, GT, SCOLS], BF16)
        maskm = sb("maskm", [P, 2, TILES, QM], BF16)
        prods = sb("prods", [P, TILES * QM], F32)
        prod = prods[:, 0:GT * SCOLS].rearrange("p (t c) -> p t c", t=GT)
        prodm = prods[:, :].rearrange("p (t q) -> p t q", t=TILES)
        s = sb("s", [P, TILES, FIELDS], F32)
        dense_sb = sb("dense_sb", [P, TILES, DENSE], F32)
        zT = sb("zT", [P, 2, KE, GB], F32)
        w1_sb = sb("w1_sb", [P, K1 // P, H1], F32)
        w2_sb = sb("w2_sb", [P, H1 // P, H2], F32)
        w3_sb = sb("w3_sb", [P, H2 // P], F32)
        b1_sb = sb("b1_sb", [P, MT1], F32)
        b2_sb = sb("b2_sb", [P, MT2], F32)
        y_sb = sb("y_sb", [P, TILES], F32)

        psD = ps("psD", [P, 3, 512])
        psL = ps("psL", [P, 2, 512])
        psZ = ps("psZ", [P, 1, 512])
        psH = ps("psH", [P, 2, 512])
        psY = psL[:, 0, 0:TILES]

        d_ids = sem("d_ids")
        d_q = sem("d_q")
        d_const = sem("d_const")
        d_dense = sem("d_dense")
        d_small = [sem(f"d_small{c}") for c in range(CHUNKS)]
        d_mid = [sem(f"d_mid{k}") for k in range(NMID)]
        d_w1 = sem("d_w1")
        d_w2 = sem("d_w2")
        d_vec = sem("d_vec")
        d_first = sem("d_first")
        d_rows = [sem(f"d_rows{g}") for g in range(GROUPS)]
        d_out = sem("d_out")
        ident_zero = sem("ident_zero")
        ident_ready = sem("ident_ready")
        chain = sem("chain")
        feat_ready = sem("feat_ready")
        featT_done = sem("featT_done")
        featT_copied = sem("featT_copied")
        dist_done = sem("dist_done")
        hot_done = sem("hot_done")
        small_summed = sem("small_summed")
        mid_summed = sem("mid_summed")
        parts_ready = sem("parts_ready")
        mparts_ready = sem("mparts_ready")
        picked = sem("picked")
        taken = sem("taken")
        rows_summed = sem("rows_summed")
        zE_ready = sem("zE_ready")
        zL_ready = sem("zL_ready")
        zT_done = sem("zT_done")
        zT_copied = sem("zT_copied")
        h_done = sem("h_done")
        part_copied = sem("part_copied")
        h1_added = sem("h1_added")
        h1_ready = sem("h1_ready")
        h2_ready = sem("h2_ready")
        y_done = sem("y_done")
        y_copied = sem("y_copied")

        def z_bank(u, c):
            return psZ[:, 0, :] if u < GROUPS or c == 0 else psD[:, 0, :]

        block = ctx.enter_context(nc.Block())

        @block.sync
        def _(sp):
            sp.dma_start(ids_sb[:, :, :], ids).then_inc(d_ids, 16)
            sp.dma_start(q_sb[:, :, :], qconst).then_inc(d_q, 16)
            sp.dma_start(hotc_sb[:, :], hotc).then_inc(d_const, 16)
            sp.dma_start(maskc_sb[:, :], maskc).then_inc(d_const, 16)
            for c in range(CHUNKS):
                n = CROWS * D
                sp.dma_start(lot[:, c * n:(c + 1) * n], small[:, c * n:(c + 1) * n]).then_inc(d_small[c], 16)
            sp.wait_ge(featT_done, len(FEAT_BANKS))
            for k in range(NMID):
                if k >= 2:
                    sp.wait_ge(mid_summed, k - 1)
                sp.dma_start(slots[:, k % 2, :], mids[k]).then_inc(d_mid[k], 16)
                if k == 0:
                    sp.dma_start(dense_sb[:, :, :], dense).then_inc(d_dense, 16)
                    sp.dma_start(b1_sb[:, :], b1).then_inc(d_vec, 16)
                    sp.dma_start(b2_sb[:, :], b2).then_inc(d_vec, 16)
                    sp.dma_start(w3_sb[:, :], w3).then_inc(d_vec, 16)
                    sp.dma_start(w1_sb[:, :, :], w1).then_inc(d_w1, 16)
                if k == 2:
                    sp.dma_start(w2_sb[:, :, :], w2).then_inc(d_w2, 16)
            sp.wait_ge(y_copied, 1)
            sp.dma_start(out, y_sb[:, :]).then_inc(d_out, 16)
            sp.wait_ge(d_out, 16)

        @block.gpsimd
        def _(pool):
            pool.memset(ident[:, :], 0.0).then_inc(ident_zero, 1)
            pool.memset(identb[:, :], 0.0).then_inc(ident_zero, 1)
            pool.wait_ge(ident_zero, 2)
            for m in (identb, ident):
                pool.affine_select(out=m[:, :], in_=m[:, :], compare_op=ALU.not_equal, fill=1.0, base=0,
                                   pattern=[[-1, P]], channel_multiplier=1).then_inc(ident_ready, 1)
            pool.wait_ge(d_ids, 16)

            def gather(dst, f, t, landed):
                pool.indirect_dma_start(
                    out=dst, out_offset=None, in_=big[f],
                    in_offset=bass.IndirectOffsetOnAxis(
                        ap=ids_sb[:, t, NSTREAM + f:NSTREAM + f + 1].bitcast(U32), axis=0),
                ).then_inc(landed, 16)

            for t in range(TILES):
                for f in range(NFIRST):
                    gather(rows_first[:, t * NFIRST + f, :], f, t, d_first)
            for g in range(GROUPS):
                if g == 1:
                    pool.wait_ge(picked, picks_after(("small", 1)))
                if g >= 2:
                    pool.wait_ge(rows_summed, g - 1)
                for t in range(GT):
                    for f in range(NLAST):
                        gather(rows[g % 2][:, t * NLAST + f, :], NFIRST + f, g * GT + t, d_rows[g])

        @block.scalar
        def _(act):
            n = 0

            def copy_feat(i):
                which, t0, nt = FEAT_BANKS[i]
                act.wait_ge(featT_done, i + 1)
                act.activation((featAT, featBT)[which][:, t0 * P:(t0 + nt) * P],
                               psH[0:FPAD, i % 2, :].bitcast(BF16)[:, 0:nt * P], ACT.Copy).then_inc(featT_copied, 1)

            def indicator(dst, cols, tiles=None):
                nonlocal n
                act.wait_ge(dist_done, n + 1)
                src = psD[:, n % 3, 0:cols]
                if tiles:
                    src = src.rearrange("p (t q) -> p t q", t=tiles)
                act.activation(dst, src, ACT.Relu, bias=1.0, scale=-1.0).then_inc(hot_done, 1)
                n += 1

            def small_hots(g):
                if g == 2:
                    act.wait_ge(small_summed, CHUNKS)
                for k in range(PACKS):
                    indicator(hots[g][:, k, :], GB)
                if g >= 2:
                    act.wait_ge(taken, picks_after(("small", g - 2)))
                for t in range(GT):
                    indicator(masks[:, g % 2, t, :], SCOLS)

            def mid_hots(k):
                if k >= 2:
                    act.wait_ge(taken, picks_after(("mid", k - 2)))
                for g in range(GROUPS):
                    indicator(hotm[:, k % 2, g * GB:(g + 1) * GB], GB)
                for g in range(GROUPS):
                    indicator(maskm[:, k % 2, g * GT:(g + 1) * GT, :], GT * QM, GT)

            def copy_zT(u, c):
                if u >= 2:
                    act.wait_ge(h_done, l1_done(u - 2))
                act.wait_ge(zT_done, u * KE + c + 1)
                act.activation(zT[:, u % 2, c, :], z_bank(u, c), ACT.Copy).then_inc(zT_copied, 1)

            def early_part(u):
                for m in range(MT1):
                    act.wait_ge(h_done, MT1 * u + m + 1)
                    act.activation(h1part[:, m, u * GB:(u + 1) * GB], psH[:, (MT1 * u + m) % 2, :], ACT.Identity,
                                   bias=b1_sb[:, m:m + 1]).then_inc(part_copied, 1)
                    if u + 1 < GROUPS and m < KE:
                        copy_zT(u + 1, m)

            for i in range(len(FEAT_BANKS)):
                copy_feat(i)
            for kind, i in HOT_ORDER:
                if kind == "small":
                    small_hots(i)
                elif i < 2:
                    mid_hots(i)
            act.wait_ge(d_vec, 48)
            for c in range(KE):
                copy_zT(0, c)
            for g in range(GROUPS):
                early_part(g)
                if g + 2 < NMID:
                    mid_hots(g + 2)
            for c in range(KE):
                copy_zT(GROUPS, c)
            for g in range(GROUPS):
                for m in range(MT1):
                    act.wait_ge(h1_added, MT1 * g + m + 1)
                    act.activation(h1T[:, g % 2, m, :], h1T[:, g % 2, m, :], ACT.Relu).then_inc(h1_ready, 1)
                if g >= 1:
                    act.wait_ge(y_done, g)
                for m in range(MT2):
                    n_h = l1_done(GROUPS + g) + m
                    act.wait_ge(h_done, n_h + 1)
                    act.activation(h2T[:, m, :], psH[:, n_h % 2, :], ACT.Relu,
                                   bias=b2_sb[:, m:m + 1]).then_inc(h2_ready, 1)
                    if m == 0 and g + 1 < GROUPS:
                        for c in range(KE):
                            copy_zT(GROUPS + g + 1, c)
            act.wait_ge(y_done, GROUPS)
            act.activation(y_sb[:, :], psY, ACT.Copy).then_inc(y_copied, 1)

        @block.vector
        def _(dve):
            v = nc.vector
            done = [0]

            def link(ins):
                done[0] += 1
                ins.then_inc(chain, 1)
                dve.wait_ge(chain, done[0])

            for ft in (featA, featB):
                v.memset(ft[:, :, ONE:FPAD], 1.0)
            link(v.memset(parts[:, :, :], 0.0))
            dve.wait_ge(d_ids, 16)
            dve.wait_ge(d_q, 16)

            def features(ft, t0, nt):
                x, x1, x2 = (ft[:, t0:t0 + nt, i * NSTREAM:(i + 1) * NSTREAM] for i in range(3))
                sq = tmp[2][:, t0:t0 + nt, :]
                link(v.tensor_tensor(sq, x, x, ALU.mult))
                link(v.tensor_copy(x1, sq))
                v.tensor_tensor(x2, sq, x1, ALU.subtract).then_inc(feat_ready, 1)

            for b, (t0, nt) in enumerate(FEAT_BATCHES):
                tt = slice(t0, t0 + nt)
                q_b = q_sb[:, 0, :].unsqueeze(1).to_broadcast([P, nt, NSTREAM])
                rq_b = q_sb[:, 1, :].unsqueeze(1).to_broadcast([P, nt, NSTREAM])
                raw, hi = ids_sb[:, tt, 0:NSTREAM], featA[:, tt, 0:NSTREAM]
                link(v.scalar_tensor_tensor(out=tmp[0][:, tt, :], in0=raw, scalar=0.5, in1=rq_b, op0=ALU.add,
                                            op1=ALU.mult))
                link(v.tensor_scalar(tmp[1][:, tt, :], tmp[0][:, tt, :], -0.5, MAGIC, ALU.add, ALU.add))
                link(v.tensor_scalar_add(hi, tmp[1][:, tt, :], -MAGIC))
                features(featA, t0, nt)
                link(v.tensor_tensor(tmp[0][:, tt, :], hi, q_b, ALU.mult))
                link(v.tensor_tensor(featB[:, tt, 0:NSTREAM], raw, tmp[0][:, tt, :], ALU.subtract))
                features(featB, t0, nt)

            def halves(i, half):
                pp = slice(half * HALF, (half + 1) * HALF)
                na = 2 * QA * PACKS_A
                return (parts[pp, i, 0:na].rearrange("p (k h q) -> p k h q", h=2, q=QA)[:, :, half, :],
                        parts[pp, i, na:SCOLS_PAD].rearrange("p (k h q) -> p k h q", h=2, q=QB)[:, :, half, :])

            def small_rows(x, half):
                pp = slice(half * HALF, (half + 1) * HALF)
                na = QA * PACKS_A
                return (x[pp, 0:na].rearrange("p (k q) -> p k q", q=QA),
                        x[pp, na:SROWS].rearrange("p (k q) -> p k q", q=QB))

            def split_small():
                for i, src in ((0, sums), (1, rest)):
                    for half in (0, 1):
                        for ab in (0, 1):
                            last = v.tensor_copy(halves(i, half)[ab], small_rows(src, half)[ab])
                    link(last)
                    for half in (0, 1):
                        dst = small_rows(rest, half) if i == 0 else halves(2, half)
                        for ab in (0, 1):
                            last = v.tensor_tensor(dst[ab], small_rows(src, half)[ab], halves(i, half)[ab],
                                                   ALU.subtract)
                    if i == 0:
                        link(last)
                    else:
                        last.then_inc(parts_ready, 1)

            def small_take(g):
                dve.wait_ge(hot_done, hot_after(("small", g)))
                for t in range(GT):
                    n = picks_after(("small", g)) - GT + t
                    dve.wait_ge(picked, n + 1)
                    v.tensor_tensor(prod[:, t, :], psL[:, n % 2, 0:SCOLS], masks[:, g % 2, t, :],
                                    ALU.mult).then_inc(taken, 1)
                dve.wait_ge(taken, picks_after(("small", g)))
                tt = slice(g * GT, (g + 1) * GT)
                v.reduce_sum(s[:, tt, 0:NA], prod[:, :, 0:CA_COLS].rearrange("p t (f q) -> p t f q", q=QA),
                             axis=AX.X)
                link(v.reduce_sum(s[:, tt, NA:NSMALL],
                                  prod[:, :, CA_COLS:SCOLS].rearrange("p t (f q) -> p t f q", q=QB), axis=AX.X))

            def mid_sums(k):
                dve.wait_ge(d_mid[k], 16)
                v.reduce_sum(msums[:, :], slots[:, k % 2, :].rearrange("p (r d) -> p r d", d=D),
                             axis=AX.X).then_inc(mid_summed, 1)
                dve.wait_ge(mid_summed, k + 1)
                if k >= 2:
                    dve.wait_ge(picked, picks_after(("mid", k - 2)))
                mrest = rest[:, 0:QM]
                link(v.tensor_copy(mparts[:, k % 2, 0, :], msums[:, :]))
                link(v.tensor_tensor(mrest, msums[:, :], mparts[:, k % 2, 0, :], ALU.subtract))
                link(v.tensor_copy(mparts[:, k % 2, 1, :], mrest))
                v.tensor_tensor(mparts[:, k % 2, 2, :], mrest, mparts[:, k % 2, 1, :],
                                ALU.subtract).then_inc(mparts_ready, 1)

            def mid_take(k):
                dve.wait_ge(hot_done, hot_after(("mid", k)))
                for g in range(GROUPS):
                    n = picks_after(("mid", k)) - GROUPS + g
                    dve.wait_ge(picked, n + 1)
                    tt = slice(g * GT, (g + 1) * GT)
                    v.tensor_tensor(prodm[:, tt, :], psL[:, n % 2, 0:GT * QM].rearrange("p (t q) -> p t q", t=GT),
                                    maskm[:, k % 2, tt, :], ALU.mult).then_inc(taken, 1)
                dve.wait_ge(taken, picks_after(("mid", k)))
                link(v.reduce_sum(s[:, :, MID0 + k:MID0 + k + 1], prodm, axis=AX.X))

            def first_rows():
                dve.wait_ge(d_first, 16 * TILES * NFIRST)
                link(v.reduce_sum(s[:, :, NSMALL:MID0],
                                  rows_first[:, :, :].rearrange("p (t f) d -> p t f d", t=TILES), axis=AX.X))

            def last_rows(g):
                dve.wait_ge(d_rows[g], 16 * GT * NLAST)
                v.reduce_sum(s[:, g * GT:(g + 1) * GT, LAST0:FIELDS],
                             rows[g % 2][:, :, :].rearrange("p (t f) d -> p t f d", t=GT),
                             axis=AX.X).then_inc(rows_summed, 1)
                dve.wait_ge(rows_summed, g + 1)

            def early_z():
                dve.wait_ge(d_dense, 16)
                v.tensor_copy(zE[:, :, 0:DENSE], dense_sb[:, :, :])
                for j in range(1, EARLY_J + 1):
                    n_i = min(j, EARLY - pair_col(j))
                    last = v.tensor_tensor(zE[:, :, pair_col(j):pair_col(j) + n_i], s[:, :, 0:n_i],
                                           s[:, :, j:j + 1].to_broadcast([P, TILES, n_i]), ALU.mult)
                last.then_inc(zE_ready, 1)

            def late_z(g):
                if g >= 1:
                    dve.wait_ge(zT_done, KE * (GROUPS + g))
                tt = slice(g * GT, (g + 1) * GT)
                for j in range(EARLY_J, FIELDS):
                    i0 = max(0, EARLY - pair_col(j))
                    c = pair_col(j) + i0 - EARLY
                    last = v.tensor_tensor(zL[:, :, c:c + j - i0], s[:, tt, i0:j],
                                           s[:, tt, j:j + 1].to_broadcast([P, GT, j - i0]), ALU.mult)
                last.then_inc(zL_ready, 1)

            def add_halves(g):
                if g >= 2:
                    dve.wait_ge(h_done, l1_done(GROUPS + g - 2) + MT2)
                for m in range(MT1):
                    n = l1_done(GROUPS + g) - MT1 + m
                    dve.wait_ge(h_done, n + 1)
                    if g == 0 and m == 0:
                        dve.wait_ge(part_copied, MT1 * GROUPS)
                    v.tensor_tensor(h1T[:, g % 2, m, :], psH[:, n % 2, :], h1part[:, m, g * GB:(g + 1) * GB],
                                    ALU.add).then_inc(h1_added, 1)

            for c in range(CHUNKS):
                dve.wait_ge(d_small[c], 16)
                rr = slice(c * CROWS, (c + 1) * CROWS)
                v.reduce_sum(sums[:, rr], small_sb[:, rr, :], axis=AX.X).then_inc(small_summed, 1)
            dve.wait_ge(small_summed, CHUNKS)
            split_small()
            small_take(0)
            small_take(1)
            mid_sums(0)
            small_take(2)
            small_take(3)
            first_rows()
            early_z()
            mid_take(0)
            mid_sums(1)
            mid_take(1)
            last_rows(0)
            for k in range(2, NMID):
                mid_sums(k)
                mid_take(k)
            late_z(0)
            last_rows(1)
            for g in range(GROUPS):
                if g + 1 < GROUPS - 1:
                    late_z(g + 1)
                add_halves(g)
                if g + 2 < GROUPS:
                    last_rows(g + 2)
                if g == GROUPS - 2:
                    late_z(GROUPS - 1)

        @block.tensor
        def _(pe):
            t_ = nc.tensor
            pe.wait_ge(ident_ready, 2)
            for i, (which, t0, nt) in enumerate(FEAT_BANKS):
                pe.wait_ge(feat_ready, FEAT_NEEDS[i])
                if i >= 2:
                    pe.wait_ge(featT_copied, i - 1)
                o = psH[0:FPAD, i % 2, :].bitcast(BF16)
                for t in range(nt):
                    last = t_.transpose(o[:, t * P:(t + 1) * P], (featA, featB)[which][:, t0 + t, :], identb[:, :])
                last.then_inc(featT_done, 1)
            pe.wait_ge(d_const, 32)

            nd = 0

            def dist_bank():
                nonlocal nd
                if nd >= 3:
                    pe.wait_ge(hot_done, nd - 2)
                nd += 1
                return psD[:, (nd - 1) % 3, :]

            def small_dist(g, i):
                o = dist_bank()
                if i < PACKS:
                    t_.matmul(o, hotc_sb[:, i * P:(i + 1) * P], featAT[0:FROWS, g * GB:(g + 1) * GB],
                              start=True, stop=True).then_inc(dist_done, 1)
                else:
                    c = (g * GT + i - PACKS) * P
                    t_.matmul(o[:, 0:SCOLS], featBT[0:FROWS, c:c + P], maskc_sb[:, 0:SCOLS],
                              start=True, stop=True).then_inc(dist_done, 1)

            def mid_dist(k, i):
                o = dist_bank()
                if i < GROUPS:
                    t_.matmul(o, hotc_sb[:, (PACKS + k) * P:(PACKS + k + 1) * P],
                              featAT[0:FROWS, i * GB:(i + 1) * GB], start=True, stop=True).then_inc(dist_done, 1)
                else:
                    for t in range(GT):
                        c = ((i - GROUPS) * GT + t) * P
                        last = t_.matmul(o[:, t * QM:(t + 1) * QM], featBT[0:FROWS, c:c + P],
                                         maskc_sb[:, SCOLS + k * QM:SCOLS + (k + 1) * QM], start=True, stop=True)
                    last.then_inc(dist_done, 1)

            def small_pick(g, t):
                if t == 0:
                    pe.wait_ge(hot_done, hot_before(("small", g)) + PACKS)
                n = picks_after(("small", g)) - GT + t
                if n >= 2:
                    pe.wait_ge(taken, n - 1)
                for k in range(PACKS):
                    c0, c1 = pack_span(k)
                    for i in range(3):
                        last = t_.matmul(psL[:, n % 2, c0:c1], hots[g][:, k, t * P:(t + 1) * P],
                                         parts[:, i, c0:c1], start=(i == 0), stop=(i == 2))
                last.then_inc(picked, 1)

            def mid_pick(k, g):
                if g == 0:
                    pe.wait_ge(hot_done, hot_before(("mid", k)) + GROUPS)
                    pe.wait_ge(mparts_ready, k + 1)
                n = picks_after(("mid", k)) - GROUPS + g
                pe.wait_ge(taken, n - 1)
                for t in range(GT):
                    c = (g * GT + t) * P
                    for i in range(3):
                        last = t_.matmul(psL[:, n % 2, t * QM:(t + 1) * QM], hotm[:, k % 2, c:c + P],
                                         mparts[:, k % 2, i, :], start=(i == 0), stop=(i == 2))
                last.then_inc(picked, 1)

            def transposes(u, c):
                z = zE[:, u * GT:(u + 1) * GT, :] if u < GROUPS else zL
                if u >= GROUPS and c == 0:
                    pe.wait_ge(zL_ready, u - GROUPS + 1)
                n = u * KE + c
                if u > GROUPS or (u == GROUPS and c == 0):
                    pe.wait_ge(zT_copied, n - 1 if u > GROUPS else n)
                elif u == GROUPS:
                    pe.wait_ge(hot_done, hot_after(HOT_ORDER[-1]))
                elif n >= 1:
                    pe.wait_ge(zT_copied, n)
                for t in range(GT):
                    last = t_.transpose(z_bank(u, c)[:, t * P:(t + 1) * P], z[:, t, c * P:(c + 1) * P], ident[:, :])
                last.then_inc(zT_done, 1)

            def h_bank_free(n):
                r = n - 2
                if r < 0:
                    return
                if r < MT1 * GROUPS:
                    pe.wait_ge(part_copied, r + 1)
                    return
                g, i = divmod(r - MT1 * GROUPS, MT1 + MT2)
                if i < MT1:
                    pe.wait_ge(h1_added, g * MT1 + i + 1)
                else:
                    pe.wait_ge(h2_ready, g * MT2 + i - MT1 + 1)

            def layer1(u, m):
                n = l1_done(u) - MT1 + m
                h_bank_free(n)
                k0 = 0 if u < GROUPS else KE
                for c in range(KE):
                    pe.wait_ge(zT_copied, u * KE + c + 1)
                    last = t_.matmul(psH[:, n % 2, :], w1_sb[:, k0 + c, m * P:(m + 1) * P], zT[:, u % 2, c, :],
                                     start=(c == 0), stop=(c == KE - 1))
                last.then_inc(h_done, 1)

            def layer2(g, m):
                n = l1_done(GROUPS + g) + m
                h_bank_free(n)
                for c in range(MT1):
                    pe.wait_ge(h1_ready, MT1 * g + c + 1)
                    last = t_.matmul(psH[:, n % 2, :], w2_sb[:, c, m * P:(m + 1) * P], h1T[:, g % 2, c, :],
                                     start=(c == 0), stop=(c == MT1 - 1))
                last.then_inc(h_done, 1)

            def layer3(g):
                pe.wait_ge(h2_ready, MT2 * (g + 1))
                for t in range(GT):
                    for c in range(MT2):
                        last = t_.matmul(psY[:, g * GT + t:g * GT + t + 1], h2T[:, c, t * P:(t + 1) * P],
                                         w3_sb[:, c:c + 1], start=(c == 0), stop=(c == MT2 - 1))
                last.then_inc(y_done, 1)

            def early(g):
                for m in range(MT1):
                    layer1(g, m)
                    if g + 1 < GROUPS and m < KE:
                        transposes(g + 1, m)

            NI = PACKS + GT
            pe.wait_ge(featT_copied, 2)
            for i in range(NI):
                small_dist(0, i)
            pe.wait_ge(featT_copied, len(FEAT_BANKS))
            for i in range(NI):
                small_dist(1, i)
            for i in range(2 * GROUPS):
                mid_dist(0, i)
            small_dist(2, 0)
            small_dist(2, 1)
            pe.wait_ge(parts_ready, 1)
            for i in range(2, 2 * NI):
                small_dist(2 + i // NI, i % NI)
                if i % 3 == 2 and i // 3 < 2 * GT:
                    small_pick(i // 3 // GT, i // 3 % GT)
            for i in range(2 * GROUPS):
                mid_dist(1, i)
                small_pick(2 + i // GT, i % GT)
            for g in range(GROUPS):
                mid_pick(0, g)
            pe.wait_ge(zE_ready, 1)
            pe.wait_ge(d_w1, 16)
            for c in range(KE):
                transposes(0, c)
            for g in range(GROUPS):
                early(g)
                if g + 2 < NMID:
                    for i in range(2 * GROUPS):
                        mid_dist(g + 2, i)
                if g + 1 < NMID:
                    for i in range(GROUPS):
                        mid_pick(g + 1, i)
            pe.wait_ge(d_w2, 16)
            for c in range(KE):
                transposes(GROUPS, c)
            pe.wait_ge(taken, picks_after(("mid", NMID - 1)))
            for g in range(GROUPS):
                for m in range(MT1):
                    layer1(GROUPS + g, m)
                    if m == 0 and g >= 1:
                        layer3(g - 1)
                layer2(g, 0)
                if g + 1 < GROUPS:
                    for c in range(KE):
                        transposes(GROUPS + g + 1, c)
                layer2(g, 1)
            layer3(GROUPS - 1)


def lookup_constants(bf16):
    q = np.array(Q, np.float32)
    qconst = np.ascontiguousarray(np.broadcast_to(np.stack([q, 1.0 / q])[None], (P, 2, NSTREAM)), np.float32)

    def columns(field_of, k_of):
        n = len(k_of)
        c = np.zeros((FROWS, n), np.float32)
        for col in range(n):
            f, k = field_of[col], k_of[col]
            if f is None:
                c[ONE, col] = 4.0
                continue
            c[f, col] = -2.0 * k
            c[NSTREAM + f, col] = 1.0
            c[2 * NSTREAM + f, col] = 1.0
            high = float(np.float32(k * k).astype(bf16))
            c[ONE, col] = high
            c[ONE + 1, col] = k * k - high
        return c.astype(bf16)

    f_hot, k_hot = [], []
    for pack in range(PACKS):
        for half in (0, 1):
            f = 2 * pack + half
            f_hot += [f if f < NSMALL else None] * HALF
            k_hot += list(range(HALF))
    for m in range(NMID):
        f_hot += [NSMALL + m] * P
        k_hot += list(range(P))
    f_mask = [f for f in range(NSTREAM) for _ in range(Q[f])]
    k_mask = [k for f in range(NSTREAM) for k in range(Q[f])]
    return qconst, columns(f_hot, k_hot), columns(f_mask, k_mask)


def kernel(**inputs):
    import ml_dtypes
    import concourse.bacc as _bacc
    from concourse import mybir as _mybir
    from concourse.bass_utils import run_bass_kernel_spmd as _run

    def arr(name):
        return np.asarray(inputs[name])

    def padded(f, parts, q):
        t = arr(f"tbl_{f}")
        full = np.zeros((parts * q, D), t.dtype)
        full[:t.shape[0]] = t
        return full.reshape(parts, q * D)

    qconst, hotc, maskc = lookup_constants(ml_dtypes.bfloat16)
    small = []
    for pack in range(PACKS):
        q = QA if pack < PACKS_A else QB
        pair = [padded(SMALL[f], HALF, q) if f < NSMALL else np.zeros((HALF, q * D), np.float32)
                for f in (2 * pack, 2 * pack + 1)]
        small.append(np.concatenate(pair))
    first = [i * (2 * FIELDS - 1 - i) // 2 for i in range(FIELDS)]
    n_pairs = K1 - DENSE
    rows = list(range(n_pairs, K1))
    for j in range(1, FIELDS):
        for i in range(j):
            a, b = sorted((ORDER[i], ORDER[j]))
            rows.append(first[a] + b - a - 1)
    arrays = {
        "dense": arr("dense_ctx").reshape(P, TILES, DENSE),
        "ids": arr("ids")[:, SMALL + MIDDLE[:NMID] + GATHERED].reshape(P, TILES, FIELDS),
        "qconst": qconst, "hotc": hotc, "maskc": maskc,
        "small": np.concatenate(small, axis=1),
    }
    for k in range(NMID):
        arrays[f"mid{k}"] = padded(MIDDLE[k], P, QM)
    for n, f in enumerate(GATHERED):
        arrays[f"big{n}"] = arr(f"tbl_{f}")
    arrays["w1"] = arr("W_top1")[rows].reshape(K1 // P, P, H1).transpose(1, 0, 2)
    arrays["b1"] = arr("b_top1").reshape(MT1, P).T
    arrays["w2"] = arr("W_top2").reshape(MT1, P, H2).transpose(1, 0, 2)
    arrays["b2"] = arr("b_top2").reshape(MT2, P).T
    arrays["w3"] = arr("W_top3").reshape(MT2, P).T
    arrays = {k: np.ascontiguousarray(a) for k, a in arrays.items()}

    nc = _bacc.Bacc("TRN2", target_bir_lowering=False, num_devices=1)
    ap = {k: nc.dram_tensor(f"in_{k}", a.shape, _mybir.dt.from_np(a.dtype), kind="ExternalInput").ap()
          for k, a in arrays.items()}
    out = nc.dram_tensor("out_y", (P, TILES), _mybir.dt.float32, kind="ExternalOutput").ap()
    dlrm_tower(nc, ap["dense"], ap["ids"], ap["qconst"], ap["hotc"], ap["maskc"], ap["small"],
               [ap[f"mid{k}"] for k in range(NMID)], [ap[f"big{n}"] for n in range(len(GATHERED))],
               ap["w1"], ap["b1"], ap["w2"], ap["b2"], ap["w3"], out)
    r = _run(nc, [{f"in_{k}": a for k, a in arrays.items()}], core_ids=[0])
    return np.asarray(r.results[0]["out_y"]).reshape(BATCH, 1)
```

```python
from contextlib import ExitStack

import numpy as np

import concourse.bass as bass
from concourse import mybir

F32 = mybir.dt.float32
BF16 = mybir.dt.bfloat16
I32 = mybir.dt.int32
U32 = mybir.dt.uint32
ALU = mybir.AluOpType
ACT = mybir.ActivationFunctionType
AX = mybir.AxisListType

P = 128
BATCH = 2048
D = 64
TILES = BATCH // P
GROUPS = 4
GT = TILES // GROUPS
GB = GT * P

ROWS = [1250, 1250, 125000, 1250, 1250, 1250, 1000, 12500, 1000, 1000, 1250, 125000, 125000, 12500, 12500,
        12500, 12500, 1000, 1000, 1250, 1000, 1250, 1250, 12500, 1000, 12500, 1000, 12500, 1000, 1000, 1000, 1000]
FIELDS = len(ROWS)

NMID = 3
SMALL = sorted((f for f in range(FIELDS) if ROWS[f] < 2000), key=lambda f: -ROWS[f])
MIDDLE = [f for f in range(FIELDS) if 2000 <= ROWS[f] < 20000]
LARGE = [f for f in range(FIELDS) if ROWS[f] >= 20000]
GATHERED = LARGE + MIDDLE[NMID:]
NSMALL = len(SMALL)
NSTREAM = NSMALL + NMID
NFIRST = 2
NLAST = len(GATHERED) - NFIRST
ORDER = SMALL + GATHERED[:NFIRST] + MIDDLE[:NMID - 1] + GATHERED[NFIRST:] + [MIDDLE[NMID - 1]]
MID0 = NSMALL + NFIRST
LAST0 = MID0 + NMID - 1

HALF = P // 2
QA, QB = 20, 16
PACKS_A = -(-sum(ROWS[f] > HALF * QB for f in SMALL) // 2)
PACKS_B = -(-(NSMALL - 2 * PACKS_A) // 2)
PACKS = PACKS_A + PACKS_B
NA, NB = 2 * PACKS_A, NSMALL - 2 * PACKS_A
SROWS = PACKS_A * QA + PACKS_B * QB
CA_COLS = NA * QA
SCOLS = CA_COLS + NB * QB
SCOLS_PAD = 2 * SROWS
CHUNKS = 4
CROWS = SROWS // CHUNKS
QM = -(-12500 // P)
SLOT = QM * D
assert SROWS == 2 * QM and SROWS % CHUNKS == 0 and QA * HALF >= 1250 and QB * HALF >= 1000

Q = [QA] * NA + [QB] * NB + [QM] * NMID
FROWS = 3 * NSTREAM + 2
FPAD = 96
ONE = 3 * NSTREAM
assert FROWS <= FPAD

FEAT_BATCHES = [(0, GT), (GT, TILES - GT)]
FEAT_BANKS = [(0, 0, GT), (1, 0, GT), (0, GT, 6), (0, GT + 6, 6), (1, GT, 6), (1, GT + 6, 6)]
FEAT_NEEDS = [1, 2, 3, 3, 4, 4]
FEAT_BESIDE = {9: (2, 3), 12: (4, 5)}

DENSE = 16
H1, H2 = 512, 256
K1 = FIELDS * (FIELDS - 1) // 2 + DENSE
EARLY = K1 // 2
KE = EARLY // P
MT1, MT2 = H1 // P, H2 // P
EARLY_J = next(j for j in range(FIELDS) if DENSE + (j + 1) * j // 2 >= EARLY)
assert EARLY_J == NSMALL + 1 and K1 == 512 and KE == 2 and NMID == 3
MAGIC = 1.5 * 2.0 ** 23


def pair_col(j):
    return DENSE + j * (j - 1) // 2


def pack_span(k):
    if k < PACKS_A:
        return 2 * QA * k, 2 * QA * (k + 1)
    a = CA_COLS + 2 * QB * (k - PACKS_A)
    return a, min(a + 2 * QB, SCOLS)


HOT_ORDER = [("small", g) for g in range(GROUPS)] + [("mid", k) for k in range(NMID)]
PICK_ORDER = [("small", g) for g in range(GROUPS)] + [("mid", k) for k in range(NMID)]


def hot_before(item):
    return sum((PACKS + GT) if kind == "small" else 2 * GROUPS for kind, _ in HOT_ORDER[:HOT_ORDER.index(item)])


def hot_after(item):
    return hot_before(item) + ((PACKS + GT) if item[0] == "small" else 2 * GROUPS)


def picks_after(item):
    return GROUPS * (PICK_ORDER.index(item) + 1)


def mid_hots_beside(g, m):
    k = (0, 1, NMID, 2)[g]
    return [(k, i) for i in (2 * m, 2 * m + 1)] if k < NMID else []


MID_PICKS = {(2, 1): 0, (2, 2): 1, (3, 3): 2}


def l1_done(u):
    return MT1 * (u + 1) if u < GROUPS else MT1 * GROUPS + (MT1 + MT2) * (u - GROUPS) + MT1


def dlrm_tower(nc, dense, ids, qconst, hotc, maskc, small, mids, big, w1, b1, w2, b2, w3, out):
    ctx = ExitStack()
    with ctx:
        def sb(name, shape, dt):
            return ctx.enter_context(nc.sbuf_tensor(name, shape, dt))

        def ps(name, shape, dt=F32):
            return ctx.enter_context(nc.psum_tensor(name, shape, dt))

        def sem(name):
            return ctx.enter_context(nc.semaphore(name))

        slots = sb("slots", [P, 2, SLOT], F32)
        lot = sb("lot", [P, 2 * SLOT], F32)
        small_sb = lot[:, :].rearrange("p (r d) -> p r d", d=D)
        h1part = lot[:, 0:MT1 * BATCH].rearrange("p (u m b) -> p u m b", u=GROUPS, m=MT1)
        h1T = lot[:, MT1 * BATCH:MT1 * BATCH + 2 * MT1 * GB].rearrange("p (u m b) -> p u m b", u=2, m=MT1)
        n_ft = TILES * FPAD // 2
        featA, featB = (slots[:, 1, i * n_ft:(i + 1) * n_ft].bitcast(BF16).rearrange(
            "p (t f) -> p t f", t=TILES) for i in (0, 1))
        n_id = TILES * NSTREAM
        tmp = [slots[:, 0, i * n_id:(i + 1) * n_id].rearrange("p (t f) -> p t f", t=TILES) for i in range(3)]
        h2T = slots[:, 1, 0:MT2 * GB].rearrange("p (m b) -> p m b", m=MT2)
        zL = slots[:, 1, MT2 * GB:MT2 * GB + GT * EARLY].rearrange("p (t k) -> p t k", t=GT)

        ids_sb = sb("ids_sb", [P, TILES, FIELDS], I32)
        q_sb = sb("q_sb", [P, 2, NSTREAM], F32)
        featAT = sb("featAT", [FPAD, BATCH], BF16)
        featBT = sb("featBT", [FPAD, BATCH], BF16)
        hotc_sb = sb("hotc_sb", [FROWS, (PACKS + NMID) * P], BF16)
        maskc_sb = sb("maskc_sb", [FROWS, SCOLS + NMID * QM], BF16)
        ident = sb("ident", [P, P], F32)
        identb = sb("identb", [P, P], BF16)
        sums = sb("sums", [P, SROWS], F32)
        rest = sb("rest", [P, SROWS], F32)
        parts = sb("parts", [P, 3, SCOLS_PAD], BF16)
        msums = sb("msums", [P, QM], F32)
        mparts = sb("mparts", [P, 2, 3, QM], BF16)
        n_hot = PACKS * GB // 2
        area = sb("area", [P, 2 * n_hot], F32)
        hot_at = (0, n_hot, 2 * SLOT - 2 * n_hot, 2 * SLOT - n_hot)
        assert hot_at[2] >= (GROUPS - 1) * MT1 * GB
        hots = [(area, area, lot, lot)[g][:, hot_at[g]:hot_at[g] + n_hot].bitcast(BF16).rearrange(
            "p (k b) -> p k b", k=PACKS) for g in range(GROUPS)]
        zE = area[:, 0:TILES * EARLY].rearrange("p (t k) -> p t k", t=TILES)
        n_row = GT * NLAST * D
        rows_even = sb("rows_even", [P, GT * NLAST, D], F32)
        rows_odd = area[:, TILES * EARLY:TILES * EARLY + n_row].rearrange("p (r d) -> p r d", d=D)
        rows = [rows_even, rows_odd]
        rows_first = sb("rows_first", [P, TILES * NFIRST, D], F32)
        hotm = sb("hotm", [P, 2, BATCH], BF16)
        masks = sb("masks", [P, 2, GT, SCOLS], BF16)
        maskm = sb("maskm", [P, 2, TILES, QM], BF16)
        prods = sb("prods", [P, TILES * QM], F32)
        prod = prods[:, 0:GT * SCOLS].rearrange("p (t c) -> p t c", t=GT)
        prodm = prods[:, :].rearrange("p (t q) -> p t q", t=TILES)
        s = sb("s", [P, TILES, FIELDS], F32)
        dense_sb = sb("dense_sb", [P, TILES, DENSE], F32)
        zT = sb("zT", [P, 2, KE, GB], F32)
        w1_sb = sb("w1_sb", [P, K1 // P, H1], F32)
        w2_sb = sb("w2_sb", [P, H1 // P, H2], F32)
        w3_sb = sb("w3_sb", [P, H2 // P], F32)
        b1_sb = sb("b1_sb", [P, MT1], F32)
        b2_sb = sb("b2_sb", [P, MT2], F32)
        y_sb = sb("y_sb", [P, TILES], F32)

        psD = ps("psD", [P, 3, 512])
        psL = ps("psL", [P, 2, 512])
        psZ = ps("psZ", [P, 1, 512])
        psH = ps("psH", [P, 2, 512])
        psY = psL[:, 0, 0:TILES]

        d_ids = sem("d_ids")
        d_q = sem("d_q")
        d_const = sem("d_const")
        d_dense = sem("d_dense")
        d_small = [sem(f"d_small{c}") for c in range(CHUNKS)]
        d_mid = [sem(f"d_mid{k}") for k in range(NMID)]
        d_w1 = sem("d_w1")
        d_w2 = sem("d_w2")
        d_vec = sem("d_vec")
        d_first = [sem(f"d_first{h}") for h in (0, 1)]
        d_rows = [sem(f"d_rows{g}") for g in range(GROUPS)]
        d_out = sem("d_out")
        ident_zero = sem("ident_zero")
        ident_ready = sem("ident_ready")
        chain = sem("chain")
        feat_ready = sem("feat_ready")
        featT_done = sem("featT_done")
        featT_copied = sem("featT_copied")
        dist_done = sem("dist_done")
        hot_done = sem("hot_done")
        small_summed = sem("small_summed")
        mid_summed = sem("mid_summed")
        parts_ready = sem("parts_ready")
        mparts_ready = sem("mparts_ready")
        picked = sem("picked")
        taken = sem("taken")
        rows_summed = sem("rows_summed")
        zE_ready = sem("zE_ready")
        zL_body = sem("zL_body")
        zL_ready = sem("zL_ready")
        zT_done = sem("zT_done")
        zT_copied = sem("zT_copied")
        h_done = sem("h_done")
        part_copied = sem("part_copied")
        h1_added = sem("h1_added")
        h1_ready = sem("h1_ready")
        h2_ready = sem("h2_ready")
        y_done = sem("y_done")
        y_copied = sem("y_copied")

        def z_bank(u, c):
            return psZ[:, 0, :] if u < GROUPS or c == 0 else psD[:, 0, :]

        block = ctx.enter_context(nc.Block())

        @block.sync
        def _(sp):
            sp.dma_start(ids_sb[:, :, :], ids).then_inc(d_ids, 16)
            sp.dma_start(q_sb[:, :, :], qconst).then_inc(d_q, 16)
            sp.dma_start(hotc_sb[:, :], hotc).then_inc(d_const, 16)
            sp.dma_start(maskc_sb[:, :], maskc).then_inc(d_const, 16)
            for c in range(CHUNKS):
                n = CROWS * D
                sp.dma_start(lot[:, c * n:(c + 1) * n], small[:, c * n:(c + 1) * n]).then_inc(d_small[c], 16)
            sp.wait_ge(featT_done, len(FEAT_BANKS))
            for k in range(NMID):
                if k == 1:
                    sp.wait_ge(d_first[0], 16 * TILES // 2 * NFIRST)
                    sp.wait_ge(d_first[1], 16 * TILES // 2 * NFIRST)
                if k >= 2:
                    sp.wait_ge(mid_summed, k - 1)
                sp.dma_start(slots[:, k % 2, :], mids[k]).then_inc(d_mid[k], 16)
                if k == 0:
                    sp.dma_start(dense_sb[:, :, :], dense).then_inc(d_dense, 16)
                    sp.dma_start(b1_sb[:, :], b1).then_inc(d_vec, 16)
                    sp.dma_start(b2_sb[:, :], b2).then_inc(d_vec, 16)
                    sp.dma_start(w3_sb[:, :], w3).then_inc(d_vec, 16)
                    sp.dma_start(w1_sb[:, :, :], w1).then_inc(d_w1, 16)
                if k == 2:
                    sp.dma_start(w2_sb[:, :, :], w2).then_inc(d_w2, 16)
            sp.wait_ge(y_copied, 1)
            sp.dma_start(out, y_sb[:, :]).then_inc(d_out, 16)
            sp.wait_ge(d_out, 16)

        @block.gpsimd
        def _(pool):
            pool.memset(ident[:, :], 0.0).then_inc(ident_zero, 1)
            pool.memset(identb[:, :], 0.0).then_inc(ident_zero, 1)
            pool.wait_ge(ident_zero, 2)
            for m in (identb, ident):
                pool.affine_select(out=m[:, :], in_=m[:, :], compare_op=ALU.not_equal, fill=1.0, base=0,
                                   pattern=[[-1, P]], channel_multiplier=1).then_inc(ident_ready, 1)
            pool.wait_ge(d_ids, 16)

            def gather(dst, f, t, landed):
                pool.indirect_dma_start(
                    out=dst, out_offset=None, in_=big[f],
                    in_offset=bass.IndirectOffsetOnAxis(
                        ap=ids_sb[:, t, NSTREAM + f:NSTREAM + f + 1].bitcast(U32), axis=0),
                ).then_inc(landed, 16)

            for t in range(TILES):
                for f in range(NFIRST):
                    gather(rows_first[:, t * NFIRST + f, :], f, t, d_first[t // (TILES // 2)])
            for g in range(GROUPS):
                if g == 1:
                    pool.wait_ge(picked, picks_after(("small", 1)))
                if g >= 2:
                    pool.wait_ge(rows_summed, g - 1)
                for t in range(GT):
                    for f in range(NLAST):
                        gather(rows[g % 2][:, t * NLAST + f, :], NFIRST + f, g * GT + t, d_rows[g])

        @block.scalar
        def _(act):
            n = 0

            def copy_feat(i):
                which, t0, nt = FEAT_BANKS[i]
                act.wait_ge(featT_done, i + 1)
                act.activation((featAT, featBT)[which][:, t0 * P:(t0 + nt) * P],
                               psH[0:FPAD, i % 2, :].bitcast(BF16)[:, 0:nt * P], ACT.Copy).then_inc(featT_copied, 1)

            def indicator(dst, cols, tiles=None):
                nonlocal n
                act.wait_ge(dist_done, n + 1)
                src = psD[:, n % 3, 0:cols]
                if tiles:
                    src = src.rearrange("p (t q) -> p t q", t=tiles)
                act.activation(dst, src, ACT.Relu, bias=1.0, scale=-1.0).then_inc(hot_done, 1)
                n += 1

            def small_hot(g, i):
                if g == 2 and i == 0:
                    act.wait_ge(small_summed, CHUNKS)
                if g >= 2 and i == PACKS:
                    act.wait_ge(taken, picks_after(("small", g - 2)))
                if i < PACKS:
                    indicator(hots[g][:, i, :], GB)
                else:
                    indicator(masks[:, g % 2, i - PACKS, :], SCOLS)

            def mid_hot(k, i):
                if k >= 2 and i == 0:
                    act.wait_ge(taken, picks_after(("mid", k - 2)))
                if i < GROUPS:
                    indicator(hotm[:, k % 2, i * GB:(i + 1) * GB], GB)
                else:
                    indicator(maskm[:, k % 2, (i - GROUPS) * GT:(i - GROUPS + 1) * GT, :], GT * QM, GT)

            def copy_zT(u, c):
                if u >= 2:
                    act.wait_ge(h_done, l1_done(u - 2))
                act.wait_ge(zT_done, u * KE + c + 1)
                act.activation(zT[:, u % 2, c, :], z_bank(u, c), ACT.Copy).then_inc(zT_copied, 1)

            def early_part(u):
                for m in range(MT1):
                    for k, i in mid_hots_beside(u, m):
                        mid_hot(k, i)
                    act.wait_ge(h_done, MT1 * u + m + 1)
                    act.activation(h1part[:, u, m, :], psH[:, (MT1 * u + m) % 2, :], ACT.Identity,
                                   bias=b1_sb[:, m:m + 1]).then_inc(part_copied, 1)
                    if u + 1 < GROUPS and m >= MT1 - KE:
                        copy_zT(u + 1, m - (MT1 - KE))

            for i in (0, 1):
                copy_feat(i)
            for g in range(GROUPS):
                for i in range(PACKS + GT):
                    if g == 0 and i in FEAT_BESIDE:
                        for bank in FEAT_BESIDE[i]:
                            copy_feat(bank)
                    small_hot(g, i)
            act.wait_ge(d_vec, 48)
            for c in range(KE):
                copy_zT(0, c)
            for g in range(GROUPS):
                early_part(g)
            for c in range(KE):
                copy_zT(GROUPS, c)
            for g in range(GROUPS):
                for m in range(MT1):
                    act.wait_ge(h1_added, MT1 * g + m + 1)
                    act.activation(h1T[:, g % 2, m, :], h1T[:, g % 2, m, :], ACT.Relu).then_inc(h1_ready, 1)
                if g >= 1:
                    act.wait_ge(y_done, g)
                for m in range(MT2):
                    n_h = l1_done(GROUPS + g) + m
                    act.wait_ge(h_done, n_h + 1)
                    act.activation(h2T[:, m, :], psH[:, n_h % 2, :], ACT.Relu,
                                   bias=b2_sb[:, m:m + 1]).then_inc(h2_ready, 1)
                    if m == 0 and g + 1 < GROUPS:
                        for c in range(KE):
                            copy_zT(GROUPS + g + 1, c)
            act.wait_ge(y_done, GROUPS)
            act.activation(y_sb[:, :], psY, ACT.Copy).then_inc(y_copied, 1)

        @block.vector
        def _(dve):
            v = nc.vector
            done = [0]

            def link(ins):
                done[0] += 1
                ins.then_inc(chain, 1)
                dve.wait_ge(chain, done[0])

            for ft in (featA, featB):
                v.memset(ft[:, :, ONE:FPAD], 1.0)
            link(v.memset(parts[:, :, :], 0.0))
            dve.wait_ge(d_ids, 16)
            dve.wait_ge(d_q, 16)

            def features(ft, t0, nt):
                x, x1, x2 = (ft[:, t0:t0 + nt, i * NSTREAM:(i + 1) * NSTREAM] for i in range(3))
                sq = tmp[2][:, t0:t0 + nt, :]
                link(v.tensor_tensor(sq, x, x, ALU.mult))
                link(v.tensor_copy(x1, sq))
                v.tensor_tensor(x2, sq, x1, ALU.subtract).then_inc(feat_ready, 1)

            for b, (t0, nt) in enumerate(FEAT_BATCHES):
                tt = slice(t0, t0 + nt)
                q_b = q_sb[:, 0, :].unsqueeze(1).to_broadcast([P, nt, NSTREAM])
                rq_b = q_sb[:, 1, :].unsqueeze(1).to_broadcast([P, nt, NSTREAM])
                raw, hi = ids_sb[:, tt, 0:NSTREAM], featA[:, tt, 0:NSTREAM]
                link(v.scalar_tensor_tensor(out=tmp[0][:, tt, :], in0=raw, scalar=0.5, in1=rq_b, op0=ALU.add,
                                            op1=ALU.mult))
                link(v.tensor_scalar(tmp[1][:, tt, :], tmp[0][:, tt, :], -0.5, MAGIC, ALU.add, ALU.add))
                link(v.tensor_scalar_add(hi, tmp[1][:, tt, :], -MAGIC))
                features(featA, t0, nt)
                link(v.tensor_tensor(tmp[0][:, tt, :], hi, q_b, ALU.mult))
                link(v.tensor_tensor(featB[:, tt, 0:NSTREAM], raw, tmp[0][:, tt, :], ALU.subtract))
                features(featB, t0, nt)

            def halves(i, half):
                pp = slice(half * HALF, (half + 1) * HALF)
                na = 2 * QA * PACKS_A
                return (parts[pp, i, 0:na].rearrange("p (k h q) -> p k h q", h=2, q=QA)[:, :, half, :],
                        parts[pp, i, na:SCOLS_PAD].rearrange("p (k h q) -> p k h q", h=2, q=QB)[:, :, half, :])

            def small_rows(x, half):
                pp = slice(half * HALF, (half + 1) * HALF)
                na = QA * PACKS_A
                return (x[pp, 0:na].rearrange("p (k q) -> p k q", q=QA),
                        x[pp, na:SROWS].rearrange("p (k q) -> p k q", q=QB))

            def split_small():
                for i, src in ((0, sums), (1, rest)):
                    for half in (0, 1):
                        for ab in (0, 1):
                            last = v.tensor_copy(halves(i, half)[ab], small_rows(src, half)[ab])
                    link(last)
                    for half in (0, 1):
                        dst = small_rows(rest, half) if i == 0 else halves(2, half)
                        for ab in (0, 1):
                            last = v.tensor_tensor(dst[ab], small_rows(src, half)[ab], halves(i, half)[ab],
                                                   ALU.subtract)
                    if i == 0:
                        link(last)
                    else:
                        last.then_inc(parts_ready, 1)

            def small_take(g):
                dve.wait_ge(hot_done, hot_after(("small", g)))
                for t in range(GT):
                    n = picks_after(("small", g)) - GT + t
                    dve.wait_ge(picked, n + 1)
                    v.tensor_tensor(prod[:, t, :], psL[:, n % 2, 0:SCOLS], masks[:, g % 2, t, :],
                                    ALU.mult).then_inc(taken, 1)
                dve.wait_ge(taken, picks_after(("small", g)))
                tt = slice(g * GT, (g + 1) * GT)
                v.reduce_sum(s[:, tt, 0:NA], prod[:, :, 0:CA_COLS].rearrange("p t (f q) -> p t f q", q=QA),
                             axis=AX.X)
                link(v.reduce_sum(s[:, tt, NA:NSMALL],
                                  prod[:, :, CA_COLS:SCOLS].rearrange("p t (f q) -> p t f q", q=QB), axis=AX.X))

            def mid_sums(k):
                dve.wait_ge(d_mid[k], 16)
                v.reduce_sum(msums[:, :], slots[:, k % 2, :].rearrange("p (r d) -> p r d", d=D),
                             axis=AX.X).then_inc(mid_summed, 1)
                dve.wait_ge(mid_summed, k + 1)
                if k >= 2:
                    dve.wait_ge(picked, picks_after(("mid", k - 2)))
                mrest = rest[:, 0:QM]
                link(v.tensor_copy(mparts[:, k % 2, 0, :], msums[:, :]))
                link(v.tensor_tensor(mrest, msums[:, :], mparts[:, k % 2, 0, :], ALU.subtract))
                link(v.tensor_copy(mparts[:, k % 2, 1, :], mrest))
                v.tensor_tensor(mparts[:, k % 2, 2, :], mrest, mparts[:, k % 2, 1, :],
                                ALU.subtract).then_inc(mparts_ready, 1)

            def mid_take(k):
                dve.wait_ge(hot_done, hot_after(("mid", k)))
                for g in range(GROUPS):
                    n = picks_after(("mid", k)) - GROUPS + g
                    dve.wait_ge(picked, n + 1)
                    tt = slice(g * GT, (g + 1) * GT)
                    v.tensor_tensor(prodm[:, tt, :], psL[:, n % 2, 0:GT * QM].rearrange("p (t q) -> p t q", t=GT),
                                    maskm[:, k % 2, tt, :], ALU.mult).then_inc(taken, 1)
                    if k == NMID - 1:
                        dve.wait_ge(taken, n + 1)
                        link(v.reduce_sum(s[:, tt, FIELDS - 1:FIELDS], prodm[:, tt, :], axis=AX.X))
                        if g == 0:
                            late_pairs(0, FIELDS - 1, FIELDS, zL_ready)
                if k < NMID - 1:
                    dve.wait_ge(taken, picks_after(("mid", k)))
                    link(v.reduce_sum(s[:, :, MID0 + k:MID0 + k + 1], prodm, axis=AX.X))

            def first_rows(h):
                n_t = TILES // 2
                dve.wait_ge(d_first[h], 16 * n_t * NFIRST)
                link(v.reduce_sum(s[:, h * n_t:(h + 1) * n_t, NSMALL:MID0],
                                  rows_first[:, h * n_t * NFIRST:(h + 1) * n_t * NFIRST, :].rearrange(
                                      "p (t f) d -> p t f d", t=n_t), axis=AX.X))

            def last_rows(g):
                dve.wait_ge(d_rows[g], 16 * GT * NLAST)
                v.reduce_sum(s[:, g * GT:(g + 1) * GT, LAST0:FIELDS - 1],
                             rows[g % 2][:, :, :].rearrange("p (t f) d -> p t f d", t=GT),
                             axis=AX.X).then_inc(rows_summed, 1)
                dve.wait_ge(rows_summed, g + 1)

            def early_z(h):
                n_t = TILES // 2
                tt = slice(h * n_t, (h + 1) * n_t)
                if h == 0:
                    dve.wait_ge(d_dense, 16)
                v.tensor_copy(zE[:, tt, 0:DENSE], dense_sb[:, tt, :])
                for j in range(1, EARLY_J + 1):
                    n_i = min(j, EARLY - pair_col(j))
                    last = v.tensor_tensor(zE[:, tt, pair_col(j):pair_col(j) + n_i], s[:, tt, 0:n_i],
                                           s[:, tt, j:j + 1].to_broadcast([P, n_t, n_i]), ALU.mult)
                last.then_inc(zE_ready, 1)

            def late_pairs(g, j0, j1, ready):
                tt = slice(g * GT, (g + 1) * GT)
                for j in range(j0, j1):
                    i0 = max(0, EARLY - pair_col(j))
                    c = pair_col(j) + i0 - EARLY
                    last = v.tensor_tensor(zL[:, :, c:c + j - i0], s[:, tt, i0:j],
                                           s[:, tt, j:j + 1].to_broadcast([P, GT, j - i0]), ALU.mult)
                last.then_inc(ready, 1)

            def late_z(g):
                dve.wait_ge(zT_done, KE * (GROUPS + g))
                late_pairs(g, EARLY_J, FIELDS - 1, zL_body)
                late_pairs(g, FIELDS - 1, FIELDS, zL_ready)

            def add_half(g, m):
                if g >= 2 and m == 0:
                    dve.wait_ge(h_done, l1_done(GROUPS + g - 2) + MT2)
                n = l1_done(GROUPS + g) - MT1 + m
                dve.wait_ge(h_done, n + 1)
                if g == 0 and m == 0:
                    dve.wait_ge(part_copied, MT1 * GROUPS)
                v.tensor_tensor(h1T[:, g % 2, m, :], psH[:, n % 2, :], h1part[:, g, m, :],
                                ALU.add).then_inc(h1_added, 1)

            for c in range(CHUNKS):
                dve.wait_ge(d_small[c], 16)
                rr = slice(c * CROWS, (c + 1) * CROWS)
                v.reduce_sum(sums[:, rr], small_sb[:, rr, :], axis=AX.X).then_inc(small_summed, 1)
            dve.wait_ge(small_summed, CHUNKS)
            split_small()
            small_take(0)
            small_take(1)
            first_rows(0)
            early_z(0)
            mid_sums(0)
            small_take(2)
            small_take(3)
            first_rows(1)
            early_z(1)
            last_rows(0)
            mid_sums(1)
            mid_take(0)
            mid_take(1)
            late_pairs(0, EARLY_J, FIELDS - 1, zL_body)
            for k in range(2, NMID):
                mid_sums(k)
                mid_take(k)
            for g in range(GROUPS):
                if 1 <= g < GROUPS - 2:
                    late_z(g + 1)
                for m in range(MT1):
                    add_half(g, m)
                    if g == 0 and m == 0:
                        last_rows(1)
                    if g == 0 and m == 1:
                        late_z(1)
                if g + 2 < GROUPS:
                    last_rows(g + 2)
                if g == GROUPS - 2:
                    late_z(GROUPS - 1)

        @block.tensor
        def _(pe):
            t_ = nc.tensor
            pe.wait_ge(ident_ready, 2)

            def feat_bank(i):
                which, t0, nt = FEAT_BANKS[i]
                pe.wait_ge(feat_ready, FEAT_NEEDS[i])
                if i >= 2:
                    pe.wait_ge(featT_copied, i - 1)
                o = psH[0:FPAD, i % 2, :].bitcast(BF16)
                for t in range(nt):
                    last = t_.transpose(o[:, t * P:(t + 1) * P], (featA, featB)[which][:, t0 + t, :], identb[:, :])
                last.then_inc(featT_done, 1)

            nd = 0

            def dist_bank():
                nonlocal nd
                if nd >= 3:
                    pe.wait_ge(hot_done, nd - 2)
                nd += 1
                return psD[:, (nd - 1) % 3, :]

            def small_dist(g, i):
                o = dist_bank()
                if i < PACKS:
                    t_.matmul(o, hotc_sb[:, i * P:(i + 1) * P], featAT[0:FROWS, g * GB:(g + 1) * GB],
                              start=True, stop=True).then_inc(dist_done, 1)
                else:
                    c = (g * GT + i - PACKS) * P
                    t_.matmul(o[:, 0:SCOLS], featBT[0:FROWS, c:c + P], maskc_sb[:, 0:SCOLS],
                              start=True, stop=True).then_inc(dist_done, 1)

            def mid_dist(k, i):
                o = dist_bank()
                if i < GROUPS:
                    t_.matmul(o, hotc_sb[:, (PACKS + k) * P:(PACKS + k + 1) * P],
                              featAT[0:FROWS, i * GB:(i + 1) * GB], start=True, stop=True).then_inc(dist_done, 1)
                else:
                    for t in range(GT):
                        c = ((i - GROUPS) * GT + t) * P
                        last = t_.matmul(o[:, t * QM:(t + 1) * QM], featBT[0:FROWS, c:c + P],
                                         maskc_sb[:, SCOLS + k * QM:SCOLS + (k + 1) * QM], start=True, stop=True)
                    last.then_inc(dist_done, 1)

            def small_pick(g, t):
                if t == 0:
                    pe.wait_ge(hot_done, hot_before(("small", g)) + PACKS)
                n = picks_after(("small", g)) - GT + t
                if n >= 2:
                    pe.wait_ge(taken, n - 1)
                for k in range(PACKS):
                    c0, c1 = pack_span(k)
                    for i in range(3):
                        last = t_.matmul(psL[:, n % 2, c0:c1], hots[g][:, k, t * P:(t + 1) * P],
                                         parts[:, i, c0:c1], start=(i == 0), stop=(i == 2))
                last.then_inc(picked, 1)

            def mid_pick(k, g):
                if g == 0:
                    pe.wait_ge(hot_done, hot_before(("mid", k)) + GROUPS)
                    pe.wait_ge(mparts_ready, k + 1)
                n = picks_after(("mid", k)) - GROUPS + g
                pe.wait_ge(taken, n - 1)
                for t in range(GT):
                    c = (g * GT + t) * P
                    for i in range(3):
                        last = t_.matmul(psL[:, n % 2, t * QM:(t + 1) * QM], hotm[:, k % 2, c:c + P],
                                         mparts[:, k % 2, i, :], start=(i == 0), stop=(i == 2))
                last.then_inc(picked, 1)

            def transposes(u, c):
                z = zE[:, u * GT:(u + 1) * GT, :] if u < GROUPS else zL
                if u == 2 and c == 0:
                    pe.wait_ge(zE_ready, 2)
                if u >= GROUPS:
                    pe.wait_ge(zL_body if c == 0 else zL_ready, u - GROUPS + 1)
                n = u * KE + c
                if u > GROUPS or (u == GROUPS and c == 0):
                    pe.wait_ge(zT_copied, n - 1 if u > GROUPS else n)
                elif u == GROUPS:
                    pe.wait_ge(hot_done, hot_after(HOT_ORDER[-1]))
                elif n >= 1:
                    pe.wait_ge(zT_copied, n)
                for t in range(GT):
                    last = t_.transpose(z_bank(u, c)[:, t * P:(t + 1) * P], z[:, t, c * P:(c + 1) * P], ident[:, :])
                last.then_inc(zT_done, 1)

            def h_bank_free(n):
                r = n - 2
                if r < 0:
                    return
                if r < MT1 * GROUPS:
                    pe.wait_ge(part_copied, r + 1)
                    return
                g, i = divmod(r - MT1 * GROUPS, MT1 + MT2)
                if i < MT1:
                    pe.wait_ge(h1_added, g * MT1 + i + 1)
                else:
                    pe.wait_ge(h2_ready, g * MT2 + i - MT1 + 1)

            def layer1(u, m):
                n = l1_done(u) - MT1 + m
                h_bank_free(n)
                k0 = 0 if u < GROUPS else KE
                for c in range(KE):
                    pe.wait_ge(zT_copied, u * KE + c + 1)
                    last = t_.matmul(psH[:, n % 2, :], w1_sb[:, k0 + c, m * P:(m + 1) * P], zT[:, u % 2, c, :],
                                     start=(c == 0), stop=(c == KE - 1))
                last.then_inc(h_done, 1)

            def layer2(g, m):
                n = l1_done(GROUPS + g) + m
                h_bank_free(n)
                for c in range(MT1):
                    pe.wait_ge(h1_ready, MT1 * g + c + 1)
                    last = t_.matmul(psH[:, n % 2, :], w2_sb[:, c, m * P:(m + 1) * P], h1T[:, g % 2, c, :],
                                     start=(c == 0), stop=(c == MT1 - 1))
                last.then_inc(h_done, 1)

            def layer3(g):
                if g == 0:
                    pe.wait_ge(taken, picks_after(("mid", NMID - 1)))
                pe.wait_ge(h2_ready, MT2 * (g + 1))
                for t in range(GT):
                    for c in range(MT2):
                        last = t_.matmul(psY[:, g * GT + t:g * GT + t + 1], h2T[:, c, t * P:(t + 1) * P],
                                         w3_sb[:, c:c + 1], start=(c == 0), stop=(c == MT2 - 1))
                last.then_inc(y_done, 1)

            NI = PACKS + GT
            feat_bank(0)
            feat_bank(1)
            pe.wait_ge(d_const, 32)
            pe.wait_ge(featT_copied, 2)
            for i in range(NI):
                if i in FEAT_BESIDE:
                    for bank in FEAT_BESIDE[i]:
                        feat_bank(bank)
                small_dist(0, i)
            pe.wait_ge(featT_copied, len(FEAT_BANKS))
            for i in range(NI):
                small_dist(1, i)
            for i in range(PACKS):
                small_dist(2, i)
            pe.wait_ge(parts_ready, 1)
            for t in range(GT):
                small_pick(0, t)
            for t in range(GT):
                small_pick(1, t)
                small_dist(2, PACKS + t)
            for i in range(NI):
                small_dist(3, i)
            small_pick(2, 0)
            small_pick(2, 1)
            pe.wait_ge(zE_ready, 1)
            pe.wait_ge(d_w1, 16)
            for c in range(KE):
                transposes(0, c)
            for g in range(GROUPS):
                for m in range(MT1):
                    for k, i in mid_hots_beside(g, m):
                        mid_dist(k, i)
                    layer1(g, m)
                    if g == 0 and m == 1:
                        for t in range(2, GT):
                            small_pick(2, t)
                    if g == 0 and m == 2:
                        for t in range(GT):
                            small_pick(3, t)
                    if g + 1 < GROUPS and m >= MT1 - KE:
                        transposes(g + 1, m - (MT1 - KE))
                    if g == GROUPS - 1 and m == MT1 - 1:
                        transposes(GROUPS, 0)
                    if (g, m) in MID_PICKS:
                        for i in range(GROUPS):
                            mid_pick(MID_PICKS[g, m], i)
            pe.wait_ge(d_w2, 16)
            for c in range(1, KE):
                transposes(GROUPS, c)
            for g in range(GROUPS):
                for m in range(MT1):
                    layer1(GROUPS + g, m)
                    if m == 0 and g >= 1:
                        layer3(g - 1)
                layer2(g, 0)
                if g + 1 < GROUPS:
                    for c in range(KE):
                        transposes(GROUPS + g + 1, c)
                layer2(g, 1)
            layer3(GROUPS - 1)


def lookup_constants(bf16):
    q = np.array(Q, np.float32)
    qconst = np.ascontiguousarray(np.broadcast_to(np.stack([q, 1.0 / q])[None], (P, 2, NSTREAM)), np.float32)

    def columns(field_of, k_of):
        n = len(k_of)
        c = np.zeros((FROWS, n), np.float32)
        for col in range(n):
            f, k = field_of[col], k_of[col]
            if f is None:
                c[ONE, col] = 4.0
                continue
            c[f, col] = -2.0 * k
            c[NSTREAM + f, col] = 1.0
            c[2 * NSTREAM + f, col] = 1.0
            high = float(np.float32(k * k).astype(bf16))
            c[ONE, col] = high
            c[ONE + 1, col] = k * k - high
        return c.astype(bf16)

    f_hot, k_hot = [], []
    for pack in range(PACKS):
        for half in (0, 1):
            f = 2 * pack + half
            f_hot += [f if f < NSMALL else None] * HALF
            k_hot += list(range(HALF))
    for m in range(NMID):
        f_hot += [NSMALL + m] * P
        k_hot += list(range(P))
    f_mask = [f for f in range(NSTREAM) for _ in range(Q[f])]
    k_mask = [k for f in range(NSTREAM) for k in range(Q[f])]
    return qconst, columns(f_hot, k_hot), columns(f_mask, k_mask)


def kernel(**inputs):
    import ml_dtypes
    import concourse.bacc as _bacc
    from concourse import mybir as _mybir
    from concourse.bass_utils import run_bass_kernel_spmd as _run

    def arr(name):
        return np.asarray(inputs[name])

    def padded(f, parts, q):
        t = arr(f"tbl_{f}")
        full = np.zeros((parts * q, D), t.dtype)
        full[:t.shape[0]] = t
        return full.reshape(parts, q * D)

    qconst, hotc, maskc = lookup_constants(ml_dtypes.bfloat16)
    small = []
    for pack in range(PACKS):
        q = QA if pack < PACKS_A else QB
        pair = [padded(SMALL[f], HALF, q) if f < NSMALL else np.zeros((HALF, q * D), np.float32)
                for f in (2 * pack, 2 * pack + 1)]
        small.append(np.concatenate(pair))
    first = [i * (2 * FIELDS - 1 - i) // 2 for i in range(FIELDS)]
    n_pairs = K1 - DENSE
    rows = list(range(n_pairs, K1))
    for j in range(1, FIELDS):
        for i in range(j):
            a, b = sorted((ORDER[i], ORDER[j]))
            rows.append(first[a] + b - a - 1)
    arrays = {
        "dense": arr("dense_ctx").reshape(P, TILES, DENSE),
        "ids": arr("ids")[:, SMALL + MIDDLE[:NMID] + GATHERED].reshape(P, TILES, FIELDS),
        "qconst": qconst, "hotc": hotc, "maskc": maskc,
        "small": np.concatenate(small, axis=1),
    }
    for k in range(NMID):
        arrays[f"mid{k}"] = padded(MIDDLE[k], P, QM)
    for n, f in enumerate(GATHERED):
        arrays[f"big{n}"] = arr(f"tbl_{f}")
    arrays["w1"] = arr("W_top1")[rows].reshape(K1 // P, P, H1).transpose(1, 0, 2)
    arrays["b1"] = arr("b_top1").reshape(MT1, P).T
    arrays["w2"] = arr("W_top2").reshape(MT1, P, H2).transpose(1, 0, 2)
    arrays["b2"] = arr("b_top2").reshape(MT2, P).T
    arrays["w3"] = arr("W_top3").reshape(MT2, P).T
    arrays = {k: np.ascontiguousarray(a) for k, a in arrays.items()}

    nc = _bacc.Bacc("TRN2", target_bir_lowering=False, num_devices=1)
    ap = {k: nc.dram_tensor(f"in_{k}", a.shape, _mybir.dt.from_np(a.dtype), kind="ExternalInput").ap()
          for k, a in arrays.items()}
    out = nc.dram_tensor("out_y", (P, TILES), _mybir.dt.float32, kind="ExternalOutput").ap()
    dlrm_tower(nc, ap["dense"], ap["ids"], ap["qconst"], ap["hotc"], ap["maskc"], ap["small"],
               [ap[f"mid{k}"] for k in range(NMID)], [ap[f"big{n}"] for n in range(len(GATHERED))],
               ap["w1"], ap["b1"], ap["w2"], ap["b2"], ap["w3"], out)
    r = _run(nc, [{f"in_{k}": a for k, a in arrays.items()}], core_ids=[0])
    return np.asarray(r.results[0]["out_y"]).reshape(BATCH, 1)
```
